# Optimizing a Trainium2 kernel written in Bass

```python
import numpy as np
import jax
import jax.numpy as jnp

def _softmax(x, axis=-1):
    return jax.nn.softmax(x, axis=axis)

def _gelu(x):
    return jax.nn.gelu(x, approximate=True)

def _silu(x):
    return jax.nn.silu(x)

def _sigmoid(x):
    return jax.nn.sigmoid(x)

def _layernorm(x, axis=-1, eps=1e-05):
    m = jnp.mean(x, axis=axis, keepdims=True)
    v = jnp.var(x, axis=axis, keepdims=True)
    return (x - m) / jnp.sqrt(v + eps)

def _scatter_add(tgt, idx, src, axis=0):
    return tgt.at[idx].add(src)

def _segment_sum(src, seg, n):
    return jax.ops.segment_sum(src, seg, n)
kernel_name = 'mk_dlrm_tower_d1_rec_r8_ec3b63'

def setup_inputs(seed: int=0):
    np.random.seed(seed)
    _w = jnp.asarray

    def _rec_inputs():
        import jax
        import jax.numpy as jnp
        _tk = jax.random.key(seed)
        dense_ctx = jax.random.normal(jax.random.fold_in(_tk, 190), (2048, 16), jnp.float32)
        ids = jnp.stack([jax.random.randint(jax.random.fold_in(_tk, 200 + f), (2048,), 0, v, jnp.int32) for f, v in enumerate([125000, 12500, 1250, 125000, 12500, 12500, 125000, 12500, 1000, 125000, 1250, 12500, 125000, 1250, 12500, 12500, 1250, 12500, 12500, 1250, 1000, 125000, 1250, 12500, 12500, 1000, 1250, 125000, 12500, 1000, 12500, 1000, 1250, 12500, 12500, 1250, 125000, 1250, 12500])], axis=1)
        tbl_0 = 0.05 * jax.random.normal(jax.random.fold_in(_tk, 500 + 0), (125000, 16), jnp.float32)
        tbl_1 = 0.05 * jax.random.normal(jax.random.fold_in(_tk, 500 + 1), (12500, 16), jnp.float32)
        tbl_2 = 0.05 * jax.random.normal(jax.random.fold_in(_tk, 500 + 2), (1250, 16), jnp.float32)
        tbl_3 = 0.05 * jax.random.normal(jax.random.fold_in(_tk, 500 + 3), (125000, 16), jnp.float32)
        tbl_4 = 0.05 * jax.random.normal(jax.random.fold_in(_tk, 500 + 4), (12500, 16), jnp.float32)
        tbl_5 = 0.05 * jax.random.normal(jax.random.fold_in(_tk, 500 + 5), (12500, 16), jnp.float32)
        tbl_6 = 0.05 * jax.random.normal(jax.random.fold_in(_tk, 500 + 6), (125000, 16), jnp.float32)
        tbl_7 = 0.05 * jax.random.normal(jax.random.fold_in(_tk, 500 + 7), (12500, 16), jnp.float32)
        tbl_8 = 0.05 * jax.random.normal(jax.random.fold_in(_tk, 500 + 8), (1000, 16), jnp.float32)
        tbl_9 = 0.05 * jax.random.normal(jax.random.fold_in(_tk, 500 + 9), (125000, 16), jnp.float32)
        tbl_10 = 0.05 * jax.random.normal(jax.random.fold_in(_tk, 500 + 10), (1250, 16), jnp.float32)
        tbl_11 = 0.05 * jax.random.normal(jax.random.fold_in(_tk, 500 + 11), (12500, 16), jnp.float32)
        tbl_12 = 0.05 * jax.random.normal(jax.random.fold_in(_tk, 500 + 12), (125000, 16), jnp.float32)
        tbl_13 = 0.05 * jax.random.normal(jax.random.fold_in(_tk, 500 + 13), (1250, 16), jnp.float32)
        tbl_14 = 0.05 * jax.random.normal(jax.random.fold_in(_tk, 500 + 14), (12500, 16), jnp.float32)
        tbl_15 = 0.05 * jax.random.normal(jax.random.fold_in(_tk, 500 + 15), (12500, 16), jnp.float32)
        tbl_16 = 0.05 * jax.random.normal(jax.random.fold_in(_tk, 500 + 16), (1250, 16), jnp.float32)
        tbl_17 = 0.05 * jax.random.normal(jax.random.fold_in(_tk, 500 + 17), (12500, 16), jnp.float32)
        tbl_18 = 0.05 * jax.random.normal(jax.random.fold_in(_tk, 500 + 18), (12500, 16), jnp.float32)
        tbl_19 = 0.05 * jax.random.normal(jax.random.fold_in(_tk, 500 + 19), (1250, 16), jnp.float32)
        tbl_20 = 0.05 * jax.random.normal(jax.random.fold_in(_tk, 500 + 20), (1000, 16), jnp.float32)
        tbl_21 = 0.05 * jax.random.normal(jax.random.fold_in(_tk, 500 + 21), (125000, 16), jnp.float32)
        tbl_22 = 0.05 * jax.random.normal(jax.random.fold_in(_tk, 500 + 22), (1250, 16), jnp.float32)
        tbl_23 = 0.05 * jax.random.normal(jax.random.fold_in(_tk, 500 + 23), (12500, 16), jnp.float32)
        tbl_24 = 0.05 * jax.random.normal(jax.random.fold_in(_tk, 500 + 24), (12500, 16), jnp.float32)
        tbl_25 = 0.05 * jax.random.normal(jax.random.fold_in(_tk, 500 + 25), (1000, 16), jnp.float32)
        tbl_26 = 0.05 * jax.random.normal(jax.random.fold_in(_tk, 500 + 26), (1250, 16), jnp.float32)
        tbl_27 = 0.05 * jax.random.normal(jax.random.fold_in(_tk, 500 + 27), (125000, 16), jnp.float32)
        tbl_28 = 0.05 * jax.random.normal(jax.random.fold_in(_tk, 500 + 28), (12500, 16), jnp.float32)
        tbl_29 = 0.05 * jax.random.normal(jax.random.fold_in(_tk, 500 + 29), (1000, 16), jnp.float32)
        tbl_30 = 0.05 * jax.random.normal(jax.random.fold_in(_tk, 500 + 30), (12500, 16), jnp.float32)
        tbl_31 = 0.05 * jax.random.normal(jax.random.fold_in(_tk, 500 + 31), (1000, 16), jnp.float32)
        tbl_32 = 0.05 * jax.random.normal(jax.random.fold_in(_tk, 500 + 32), (1250, 16), jnp.float32)
        tbl_33 = 0.05 * jax.random.normal(jax.random.fold_in(_tk, 500 + 33), (12500, 16), jnp.float32)
        tbl_34 = 0.05 * jax.random.normal(jax.random.fold_in(_tk, 500 + 34), (12500, 16), jnp.float32)
        tbl_35 = 0.05 * jax.random.normal(jax.random.fold_in(_tk, 500 + 35), (1250, 16), jnp.float32)
        tbl_36 = 0.05 * jax.random.normal(jax.random.fold_in(_tk, 500 + 36), (125000, 16), jnp.float32)
        tbl_37 = 0.05 * jax.random.normal(jax.random.fold_in(_tk, 500 + 37), (1250, 16), jnp.float32)
        tbl_38 = 0.05 * jax.random.normal(jax.random.fold_in(_tk, 500 + 38), (12500, 16), jnp.float32)
        _rk = jax.random.fold_in(_tk, 7)
        W_top1 = 0.0606339 * jax.random.normal(jax.random.fold_in(_tk, 801), (272, 512), jnp.float32)
        W_top2 = 0.0441942 * jax.random.normal(jax.random.fold_in(_tk, 802), (512, 256), jnp.float32)
        W_top3 = 0.0625 * jax.random.normal(jax.random.fold_in(_tk, 803), (256, 1), jnp.float32)
        b_top1 = jnp.zeros((512,), jnp.float32)
        b_top2 = jnp.zeros((256,), jnp.float32)
        return (dense_ctx, ids, tbl_0, tbl_1, tbl_2, tbl_3, tbl_4, tbl_5, tbl_6, tbl_7, tbl_8, tbl_9, tbl_10, tbl_11, tbl_12, tbl_13, tbl_14, tbl_15, tbl_16, tbl_17, tbl_18, tbl_19, tbl_20, tbl_21, tbl_22, tbl_23, tbl_24, tbl_25, tbl_26, tbl_27, tbl_28, tbl_29, tbl_30, tbl_31, tbl_32, tbl_33, tbl_34, tbl_35, tbl_36, tbl_37, tbl_38, W_top1, b_top1, W_top2, b_top2, W_top3)
    dense_ctx, ids, tbl_0, tbl_1, tbl_2, tbl_3, tbl_4, tbl_5, tbl_6, tbl_7, tbl_8, tbl_9, tbl_10, tbl_11, tbl_12, tbl_13, tbl_14, tbl_15, tbl_16, tbl_17, tbl_18, tbl_19, tbl_20, tbl_21, tbl_22, tbl_23, tbl_24, tbl_25, tbl_26, tbl_27, tbl_28, tbl_29, tbl_30, tbl_31, tbl_32, tbl_33, tbl_34, tbl_35, tbl_36, tbl_37, tbl_38, W_top1, b_top1, W_top2, b_top2, W_top3 = _rec_inputs()

    def _L0_rec_setup():
        import jax, jax.numpy as jnp
        import numpy as np
        B, M0, D = (256, 39, 16)
        CIN_SIZE = [128, 128]

        def _cin(inputs, weights):
            X0 = inputs
            Xi = inputs
            res = []
            for W in weights:
                mi = Xi.shape[1]
                z = jnp.einsum('bmd,bnd->bdmn', X0, Xi)
                z = z.reshape(z.shape[0], z.shape[1], M0 * mi)
                Xi = jnp.einsum('bdp,po->bod', z, W)
                res.append(Xi)
            res = jnp.concatenate(res, axis=1)
            return jnp.sum(res, axis=-1)
        key = jax.random.key(seed)
        k1, k2, k3 = jax.random.split(key, 3)
        inputs = jax.random.normal(k1, (B, M0, D), dtype=jnp.float32)
        W0 = jax.random.normal(k2, (M0 * M0, CIN_SIZE[0]), dtype=jnp.float32) * 0.05
        W1 = jax.random.normal(k3, (M0 * CIN_SIZE[0], CIN_SIZE[1]), dtype=jnp.float32) * 0.05
        return {'inputs': inputs, 'W0': W0, 'W1': W1}
    _L0_rec_all = _L0_rec_setup()
    _L0_rec_in = {k: v for k, v in _L0_rec_all.items() if k in ('W0', 'W1')}
    del _L0_rec_all
    return {'dense_ctx': dense_ctx, 'ids': ids, 'tbl_0': tbl_0, 'tbl_1': tbl_1, 'tbl_2': tbl_2, 'tbl_3': tbl_3, 'tbl_4': tbl_4, 'tbl_5': tbl_5, 'tbl_6': tbl_6, 'tbl_7': tbl_7, 'tbl_8': tbl_8, 'tbl_9': tbl_9, 'tbl_10': tbl_10, 'tbl_11': tbl_11, 'tbl_12': tbl_12, 'tbl_13': tbl_13, 'tbl_14': tbl_14, 'tbl_15': tbl_15, 'tbl_16': tbl_16, 'tbl_17': tbl_17, 'tbl_18': tbl_18, 'tbl_19': tbl_19, 'tbl_20': tbl_20, 'tbl_21': tbl_21, 'tbl_22': tbl_22, 'tbl_23': tbl_23, 'tbl_24': tbl_24, 'tbl_25': tbl_25, 'tbl_26': tbl_26, 'tbl_27': tbl_27, 'tbl_28': tbl_28, 'tbl_29': tbl_29, 'tbl_30': tbl_30, 'tbl_31': tbl_31, 'tbl_32': tbl_32, 'tbl_33': tbl_33, 'tbl_34': tbl_34, 'tbl_35': tbl_35, 'tbl_36': tbl_36, 'tbl_37': tbl_37, 'tbl_38': tbl_38, 'W_top1': W_top1, 'b_top1': b_top1, 'W_top2': W_top2, 'b_top2': b_top2, 'W_top3': W_top3, 'L0_rec_W0': _L0_rec_in['W0'], 'L0_rec_W1': _L0_rec_in['W1']}

def reference(dense_ctx, ids, tbl_0, tbl_1, tbl_2, tbl_3, tbl_4, tbl_5, tbl_6, tbl_7, tbl_8, tbl_9, tbl_10, tbl_11, tbl_12, tbl_13, tbl_14, tbl_15, tbl_16, tbl_17, tbl_18, tbl_19, tbl_20, tbl_21, tbl_22, tbl_23, tbl_24, tbl_25, tbl_26, tbl_27, tbl_28, tbl_29, tbl_30, tbl_31, tbl_32, tbl_33, tbl_34, tbl_35, tbl_36, tbl_37, tbl_38, W_top1, b_top1, W_top2, b_top2, W_top3, L0_rec_W0, L0_rec_W1):
    import jax
    import jax.numpy as jnp

    def _L0_rec_ref(inputs, W0, W1):
        import jax, jax.numpy as jnp
        import numpy as np
        B, M0, D = (256, 39, 16)
        CIN_SIZE = [128, 128]

        def _cin(inputs, weights):
            X0 = inputs
            Xi = inputs
            res = []
            for W in weights:
                mi = Xi.shape[1]
                z = jnp.einsum('bmd,bnd->bdmn', X0, Xi)
                z = z.reshape(z.shape[0], z.shape[1], M0 * mi)
                Xi = jnp.einsum('bdp,po->bod', z, W)
                res.append(Xi)
            res = jnp.concatenate(res, axis=1)
            return jnp.sum(res, axis=-1)
        return _cin(inputs, [W0, W1])
    e = jnp.stack([tbl_0[ids[:, 0]], tbl_1[ids[:, 1]], tbl_2[ids[:, 2]], tbl_3[ids[:, 3]], tbl_4[ids[:, 4]], tbl_5[ids[:, 5]], tbl_6[ids[:, 6]], tbl_7[ids[:, 7]], tbl_8[ids[:, 8]], tbl_9[ids[:, 9]], tbl_10[ids[:, 10]], tbl_11[ids[:, 11]], tbl_12[ids[:, 12]], tbl_13[ids[:, 13]], tbl_14[ids[:, 14]], tbl_15[ids[:, 15]], tbl_16[ids[:, 16]], tbl_17[ids[:, 17]], tbl_18[ids[:, 18]], tbl_19[ids[:, 19]], tbl_20[ids[:, 20]], tbl_21[ids[:, 21]], tbl_22[ids[:, 22]], tbl_23[ids[:, 23]], tbl_24[ids[:, 24]], tbl_25[ids[:, 25]], tbl_26[ids[:, 26]], tbl_27[ids[:, 27]], tbl_28[ids[:, 28]], tbl_29[ids[:, 29]], tbl_30[ids[:, 30]], tbl_31[ids[:, 31]], tbl_32[ids[:, 32]], tbl_33[ids[:, 33]], tbl_34[ids[:, 34]], tbl_35[ids[:, 35]], tbl_36[ids[:, 36]], tbl_37[ids[:, 37]], tbl_38[ids[:, 38]]], axis=1)
    z = _L0_rec_ref(e, L0_rec_W0, L0_rec_W1)
    z = z.reshape(z.shape[0], -1)
    h = jnp.concatenate([z, dense_ctx], axis=1)
    h = jnp.maximum(h @ W_top1 + b_top1, 0.0)
    h = jnp.maximum(h @ W_top2 + b_top2, 0.0)
    y = h @ W_top3
    return y

_drawn_inputs = setup_inputs


def setup_inputs(seed=0):
    import zlib

    import numpy as np

    out = dict(_drawn_inputs(seed))
    spreads = {'b_top1': (0.0, 0.1), 'b_top2': (0.0, 0.1)}
    factors = {'tbl_0': 4.756,
     'tbl_1': 5.219,
     'tbl_2': 4.546,
     'tbl_3': 4.908,
     'tbl_4': 4.951,
     'tbl_5': 5.202,
     'tbl_6': 4.857,
     'tbl_7': 4.769,
     'tbl_8': 5.018,
     'tbl_9': 4.456,
     'tbl_10': 5.062,
     'tbl_11': 4.931,
     'tbl_12': 4.478,
     'tbl_13': 4.342,
     'tbl_14': 4.657,
     'tbl_15': 4.834,
     'tbl_16': 5.192,
     'tbl_17': 4.833,
     'tbl_18': 4.999,
     'tbl_19': 5.133,
     'tbl_20': 4.864,
     'tbl_21': 4.894,
     'tbl_22': 4.651,
     'tbl_23': 4.649,
     'tbl_24': 4.668,
     'tbl_25': 4.448,
     'tbl_26': 5.012,
     'tbl_27': 4.999,
     'tbl_28': 4.881,
     'tbl_29': 4.755,
     'tbl_30': 4.918,
     'tbl_31': 4.565,
     'tbl_32': 5.003,
     'tbl_33': 4.999,
     'tbl_34': 4.623,
     'tbl_35': 4.825,
     'tbl_36': 4.726,
     'tbl_37': 4.898,
     'tbl_38': 5.058,
     'L0_rec_W1': 5.348}
    for name, (base, spread) in spreads.items():
        noise = np.random.default_rng([zlib.crc32(name.encode()), seed]).standard_normal(out[name].shape)
        drawn = base * np.exp(spread * noise) if base else spread * noise
        out[name] = jnp.asarray(drawn.astype(out[name].dtype))
    for name, factor in factors.items():
        out[name] = (out[name] * factor).astype(out[name].dtype)
    return out
```

```python
from contextlib import ExitStack

import concourse.bass as bass
from concourse import mybir

F32 = mybir.dt.float32
F32R = mybir.dt.float32r
I32 = mybir.dt.int32
ALU = mybir.AluOpType
ACT = mybir.ActivationFunctionType

P = 128
BATCH, FIELDS, D = 2048, 39, 16
CH = 128
TILES = BATCH // P
QUARTERS = 4
DQ = D // QUARTERS
COLS = DQ * P
SHIFTS = (FIELDS + 1) // 2
PAIRS = SHIFTS * FIELDS
CHUNKS = PAIRS // P
REST = PAIRS - CHUNKS * P
RROWS = 32
ZROW = CHUNKS * P + 3 * RROWS
EXT = FIELDS + SHIFTS - 1
GB = P // D
GROUPS = P // GB
MX = FIELDS + 1
ZBANKS = 4
FILLS = CHUNKS + 1
H1, H2 = 512, 256
PRIOR = 3
FIRST_PAIR, LAST_PAIR = 2, TILES // 2


def dlrm_tower(nc, ids, dense_ctx, tables, w0_first, w0_second, w1, w_top1, b_top1, w_top2, b_top2, w_top3, y):
    with ExitStack() as ctx:
        def sb(name, shape, dt=F32):
            return ctx.enter_context(nc.sbuf_tensor(name, shape, dt))

        def bank(name):
            return ctx.enter_context(nc.psum_tensor(name, [P, 512], F32))

        def sem(name):
            return ctx.enter_context(nc.semaphore(name))

        ids_all = sb("ids_all", [P, TILES, FIELDS], I32)
        ids_tile = [sb(f"ids_tile{u}", [P, FIELDS], I32) for u in range(2)]
        emb = [sb(f"emb{u}", [P, FIELDS, D]) for u in range(2)]
        xext = [sb(f"xext{u}", [P, D, EXT]) for u in range(2)]
        prod = [sb(f"prod{u}", [P, DQ, ZROW]) for u in range(2)]
        zt = [sb(f"zt{u}", [P, CHUNKS, COLS]) for u in range(2)]
        ztrest = [sb(f"ztrest{u}", [3 * RROWS, COLS], F32R) for u in range(2)]
        x1t = sb("x1t", [P, P, D])
        x1 = sb("x1", [P, GROUPS, CH])
        xdiag = sb("xdiag", [P, GROUPS, GB, MX])
        gt = sb("gt", [P, MX, P])
        r1 = sb("r1", [P, P])
        r2 = sb("r2", [P, P])
        h1 = sb("h1", [P, H1 // P, P])
        h2 = sb("h2", [P, H2 // P, P])
        y_sb = sb("y_sb", [1, BATCH])
        w0 = sb("w0", [P, CHUNKS, CH])
        w0b = sb("w0b", [P, CHUNKS, CH])
        w0rest = sb("w0rest", [3 * RROWS, CH])
        w0restb = sb("w0restb", [3 * RROWS, CH])
        w0restr = sb("w0restr", [3 * RROWS, CH], F32R)
        w1_sb = sb("w1_sb", [P, FIELDS, CH])
        wt1 = sb("wt1", [P, 2, H1])
        wt1c = sb("wt1c", [D, H1])
        wt2 = sb("wt2", [P, H1 // P, H2])
        wt3 = sb("wt3", [P, H2 // P, 1])
        b1_sb = sb("b1_sb", [P, H1 // P])
        b2_sb = sb("b2_sb", [P, H2 // P])
        dense = sb("dense", [P, TILES, D])
        denset = sb("denset", [D, BATCH])
        ident = sb("ident", [P, P])
        carrier = sb("carrier", [1, 1])
        xrows = nc.dram_tensor("xrows", [TILES, P, D, FIELDS], F32, kind="Internal").ap()

        zps = [bank(f"zps{k}") for k in range(ZBANKS)]
        x1ps = bank("x1ps")
        gps = [bank(f"gps{k}") for k in range(2)]
        mps = bank("mps")

        ids_in = sem("ids_in")
        ids_copied = sem("ids_copied")
        ident_made = sem("ident_made")
        diag_made = sem("diag_made")
        w0_in, w0b_in, rest_in = sem("w0_in"), sem("w0b_in"), sem("rest_in")
        w1_in, top_in, dense_in = sem("w1_in"), sem("top_in"), sem("dense_in")
        pads_made = sem("pads_made")
        w0_made = sem("w0_made")
        dense_turned, dense_copied = sem("dense_turned"), sem("dense_copied")
        emb_in = [sem(f"emb_in{u}") for u in range(2)]
        xext_made = sem("xext_made")
        rows_out = [sem(f"rows_out{u}") for u in range(2)]
        diag_in = [sem(f"diag_in{h}") for h in range(2)]
        prod_made = sem("prod_made")
        z_turned = sem("z_turned")
        zt_copied = sem("zt_copied")
        rest_split = sem("rest_split")
        x1_summed = sem("x1_summed")
        x1t_copied = sem("x1t_copied")
        x1_turned = sem("x1_turned")
        x1_copied = sem("x1_copied")
        g_summed = sem("g_summed")
        g_even, g_odd = sem("g_even"), sem("g_odd")
        r1_copied = sem("r1_copied")
        r2_summed, r2_copied = sem("r2_summed"), sem("r2_copied")
        h1_summed, h1_made = sem("h1_summed"), sem("h1_made")
        h2_summed, h2_made = sem("h2_summed"), sem("h2_made")
        y_summed, y_copied = sem("y_summed"), sem("y_copied")
        y_out = sem("y_out")

        def live(j, u, back):
            return not isinstance(j, int) or 0 <= 2 * j + u - back < TILES

        def wait(eng, semaphore, value):
            if not isinstance(value, int) or value > 0:
                eng.wait_ge(semaphore, value)

        def run(eng, step):
            for j in range(FIRST_PAIR):
                step(j, 0)
                step(j, 1)
            with eng.Fori(FIRST_PAIR, LAST_PAIR) as j:
                step(j, 0)
                step(j, 1)
            step(LAST_PAIR, 0)
            step(LAST_PAIR, 1)
            step(LAST_PAIR + 1, 0)

        block = ctx.enter_context(nc.Block())

        @block.sync
        def _(sp):
            sp.dma_start(ids_all[:], ids.rearrange("(t p) f -> p t f", p=P)).then_inc(ids_in, 16)
            sp.dma_start(w0[:], w0_first[0:CHUNKS * P, :].rearrange("(c k) n -> k c n", k=P)).then_inc(w0_in, 16)
            sp.dma_start(w0b[FIELDS:P, 0, :], w0_second[0:P - FIELDS, :]).then_inc(w0b_in, 16)
            sp.dma_start(w0b[:, 1:CHUNKS, :], w0_second[P - FIELDS:CHUNKS * P - FIELDS, :]
                         .rearrange("(c k) n -> k c n", k=P)).then_inc(w0b_in, 16)
            sp.wait_ge(pads_made, 3)
            for k in range(3):
                rows = slice(k * RROWS, k * RROWS + REST)
                sp.dma_start(w0rest[rows, :], w0_first[CHUNKS * P:PAIRS, :]).then_inc(rest_in, 16)
                sp.dma_start(w0restb[rows, :], w0_second[CHUNKS * P - FIELDS:PAIRS - FIELDS, :]).then_inc(rest_in, 16)
            sp.dma_start(dense[:], dense_ctx.rearrange("(t p) k -> p t k", p=P)).then_inc(dense_in, 16)
            sp.dma_start(wt1[:], w_top1[0:2 * CH, :].rearrange("(c k) n -> k c n", k=P)).then_inc(top_in, 16)
            sp.dma_start(wt1c[:], w_top1[2 * CH:2 * CH + D, :]).then_inc(top_in, 16)
            sp.dma_start(wt2[:], w_top2.rearrange("(c k) n -> k c n", k=P)).then_inc(top_in, 16)
            sp.dma_start(wt3[:].rearrange("k c n -> k (c n)"), w_top3).then_inc(top_in, 16)
            sp.dma_start(b1_sb[:], b_top1).then_inc(top_in, 16)
            sp.dma_start(b2_sb[:], b_top2).then_inc(top_in, 16)
            sp.dma_start(w1_sb[:], w1.rearrange("(m n) o -> n m o", m=FIELDS)).then_inc(w1_in, 16)
            sp.wait_ge(diag_made, 4)
            blocks = xrows.rearrange("t (g e) d m -> t e d g m", e=GB)

            def step(j, u):
                t = 2 * j + u
                if not live(j, u, 0):
                    return
                sp.wait_ge(xext_made, 2 * t + 2)
                sp.dma_start(xrows[bass.ds(t, 1), :, :, :].rearrange("t p d m -> (t p) d m"),
                             xext[u][:, :, 0:FIELDS]).then_inc(rows_out[u], 16)
                sp.wait_ge(rows_out[u], 16 * j + 16)
                for h in range(2):
                    if live(j, u, 1):
                        sp.wait_ge(g_summed, GROUPS * (t - 1) + (h + 1) * (GROUPS // 2))
                    half = slice(h * (GROUPS // 2), (h + 1) * (GROUPS // 2))
                    for e in range(GB):
                        sp.dma_start(xdiag[e * D:(e + 1) * D, half, e, 0:FIELDS],
                                     blocks[bass.ds(t, 1), e, :, half, :].rearrange("t d g m -> (t d) g m")
                                     ).then_inc(diag_in[h], 16)

            run(sp, step)
            sp.wait_ge(y_copied, TILES)
            sp.dma_start(y.rearrange("b o -> o b"), y_sb[:]).then_inc(y_out, 16)
            sp.wait_ge(y_out, 16)

        @block.gpsimd
        def _(pool):
            pool.memset(ident[:], 0.0).then_inc(ident_made, 1)
            pool.wait_ge(ident_made, 1)
            pool.affine_select(out=ident[:], in_=ident[:], compare_op=ALU.not_equal, fill=1.0, base=0,
                               pattern=[[-1, P]], channel_multiplier=1).then_inc(ident_made, 1)
            pool.wait_ge(ids_in, 16)

            def gather(t, u):
                pool.tensor_copy(ids_tile[u][:], ids_all[:, t, :]).then_inc(ids_copied, 1)
                pool.wait_ge(ids_copied, t + 1)
                for f in range(FIELDS):
                    pool.indirect_dma_start(emb[u][:, f, :], None, tables[f],
                                            bass.IndirectOffsetOnAxis(ap=ids_tile[u][:, f:f + 1], axis=0)
                                            ).then_inc(emb_in[u], 16)

            gather(0, 0)
            pool.memset(xdiag[:], 0.0).then_inc(diag_made, 1)
            pool.wait_ge(diag_made, 1)
            ones = xdiag[:, :, :, FIELDS]
            pool.memset(ones, 1.0).then_inc(diag_made, 1)
            pool.wait_ge(diag_made, 2)
            pool.affine_select(out=ones, in_=ones, compare_op=ALU.is_ge, fill=0.0, base=0,
                               pattern=[[0, GROUPS], [-D, GB]], channel_multiplier=1).then_inc(diag_made, 1)
            pool.wait_ge(diag_made, 3)
            pool.affine_select(out=ones, in_=ones, compare_op=ALU.is_ge, fill=0.0, base=D - 1,
                               pattern=[[0, GROUPS], [D, GB]], channel_multiplier=-1).then_inc(diag_made, 1)
            gather(1, 1)
            with pool.Fori(1, TILES // 2) as j:
                for u in range(2):
                    t = 2 * j + u
                    pool.wait_ge(xext_made, 2 * (t - 1))
                    pool.tensor_copy(ids_tile[u][:], ids_all[:, bass.ds(t, 1), :]
                                     .rearrange("p t f -> p (t f)")).then_inc(ids_copied, 1)
                    pool.wait_ge(ids_copied, t + 1)
                    pool.tensor_tensor(carrier[:], ident[0:1, 0:1], ident[0:1, 0:1], ALU.mult)
                    for f in range(FIELDS):
                        pool.indirect_dma_start(emb[u][:, f, :], None, tables[f],
                                                bass.IndirectOffsetOnAxis(ap=ids_tile[u][:, f:f + 1], axis=0)
                                                ).then_inc(emb_in[u], 16)

        @block.tensor
        def _(pe):
            pe.wait_ge(ident_made, 2)
            pe.wait_ge(dense_in, 16)
            for k in range(4):
                if k >= 2:
                    pe.wait_ge(dense_copied, k - 1)
                for a in range(4):
                    last = pe.transpose(gps[k % 2][0:D, a * P:(a + 1) * P], dense[:, 4 * k + a, :], ident[:])
                last.then_inc(dense_turned, 1)
            pe.wait_ge(dense_copied, 4)
            pe.wait_ge(w0_made, 4)
            pe.wait_ge(w1_in, 16)
            pe.wait_ge(top_in, 16 * 6)

            def turn_products(t, i, q):
                z = prod[q % 2]
                pe.wait_ge(prod_made, i + 1)
                for c in range(FILLS):
                    n = FILLS * q + c
                    wait(pe, zt_copied, FILLS * i + c + 1 - ZBANKS)
                    if (c + FILLS - ZBANKS) % FILLS == FILLS - 1:
                        wait(pe, rest_split, i)
                    out = zps[n % ZBANKS]
                    for d in range(DQ):
                        if c < CHUNKS:
                            last = pe.transpose(out[:, d * P:(d + 1) * P], z[:, d, c * P:(c + 1) * P], ident[:])
                        else:
                            last = pe.transpose(out[0:3 * RROWS, d * P:(d + 1) * P], z[:, d, CHUNKS * P:ZROW], ident[:])
                    last.then_inc(z_turned, 1)

            def layer1(i, q):
                pe.wait_ge(zt_copied, FILLS * (i + 1))
                pe.wait_ge(rest_split, i + 1)
                wait(pe, x1t_copied, i)
                for c in range(CHUNKS):
                    pe.matmul(x1ps[:], w0[:, c, :], zt[q % 2][:, c, :], start=(c == 0), stop=False)
                pe.matmul(x1ps[:], w0restr[:], ztrest[q % 2][:], start=False, stop=True).then_inc(x1_summed, 1)

            def turn_x1(t):
                pe.wait_ge(x1t_copied, QUARTERS * (t + 1))
                for k in range(4):
                    if k < 2:
                        wait(pe, g_even if k == 0 else g_odd, 8 * t)
                    else:
                        pe.wait_ge(x1_copied, 4 * t + k - 1)
                    for a in range(4):
                        g = 4 * k + a
                        group = x1t[:, g * GB:(g + 1) * GB, :].rearrange("n b d -> n (b d)")
                        last = pe.transpose(gps[k % 2][:, a * CH:(a + 1) * CH], group, ident[:])
                    last.then_inc(x1_turned, 1)

            def sum_g(t, r):
                for g in range(4 * r, 4 * r + 4):
                    if g % 4 == 0:
                        pe.wait_ge(x1_copied, 4 * t + g // 4 + 1)
                    if g % 8 == 0:
                        pe.wait_ge(diag_in[g // 8], 16 * GB * (t + 1))
                    if g < 2:
                        pe.wait_ge(x1_copied, 4 * t + 3 + g)
                    elif g % 2 == 0:
                        pe.wait_ge(g_even, 8 * t + g // 2)
                    else:
                        pe.wait_ge(g_odd, 8 * t + g // 2)
                    pe.matmul(gps[g % 2][:, 0:GB * MX], x1[:, g, :], xdiag[:, g, :, :].rearrange("p b m -> p (b m)"),
                              start=True, stop=True).then_inc(g_summed, 1)

            def layer2(t):
                pe.wait_ge(g_even, 8 * (t + 1))
                pe.wait_ge(g_odd, 8 * (t + 1))
                wait(pe, y_copied, t)
                for m in range(FIELDS):
                    last = pe.matmul(mps[:, 0:P], w1_sb[:, m, :], gt[:, m, :], start=(m == 0), stop=(m == FIELDS - 1))
                last.then_inc(r2_summed, 1)

            def top1(t):
                pe.wait_ge(r1_copied, t + 1)
                pe.wait_ge(r2_copied, t + 1)
                for k in range(H1 // P):
                    cols = slice(k * P, (k + 1) * P)
                    pe.matmul(mps[:, cols], wt1[:, 0, cols], r1[:], start=True, stop=False)
                    pe.matmul(mps[:, cols], wt1[:, 1, cols], r2[:], start=False, stop=False)
                    last = pe.matmul(mps[:, cols], wt1c[:, cols], denset[:, bass.ds(t * P, P)], start=False, stop=True)
                last.then_inc(h1_summed, 1)

            def top2(t):
                pe.wait_ge(h1_made, (H1 // P) * (t + 1))
                for k in range(H2 // P):
                    cols = slice(k * P, (k + 1) * P)
                    for c in range(H1 // P):
                        last = pe.matmul(mps[:, cols], wt2[:, c, cols], h1[:, c, :], start=(c == 0),
                                         stop=(c == H1 // P - 1))
                last.then_inc(h2_summed, 1)

            def top3(t):
                pe.wait_ge(h2_made, (H2 // P) * (t + 1))
                for c in range(H2 // P):
                    last = pe.matmul(mps[0:1, 0:P], wt3[:, c, :], h2[:, c, :], start=(c == 0), stop=(c == H2 // P - 1))
                last.then_inc(y_summed, 1)

            def step(j, u):
                t = 2 * j + u
                for q in range(QUARTERS):
                    i = QUARTERS * t + q
                    if live(j, u, 0):
                        turn_products(t, i, q)
                    if live(j, u, 0 if q else 1):
                        layer1(i - 1, (q - 1) % QUARTERS)
                    if q == 0:
                        if live(j, u, 3):
                            top3(t - 3)
                        if live(j, u, 2):
                            sum_g(t - 2, 3)
                    if q == 1:
                        if live(j, u, 2):
                            layer2(t - 2)
                        if live(j, u, 1):
                            turn_x1(t - 1)
                    if q == 2 and live(j, u, 2):
                        top1(t - 2)
                    if q == 3 and live(j, u, 2):
                        top2(t - 2)
                    if q > 0 and live(j, u, 1):
                        sum_g(t - 1, q - 1)

            run(pe, step)

        @block.scalar
        def _(act):
            def lay_out(j, u):
                t = 2 * j + u
                act.wait_ge(emb_in[u], 16 * FIELDS * (j + 1))
                wait(act, prod_made, QUARTERS * (t - 1))
                wait(act, rows_out[u], 16 * j)
                turned = emb[u][:].rearrange("b m d -> b d m")
                act.copy(xext[u][:, :, 0:FIELDS], turned).then_inc(xext_made, 1)
                act.copy(xext[u][:, :, FIELDS:EXT], turned[:, :, 0:EXT - FIELDS]).then_inc(xext_made, 1)

            def copy_g(t, r):
                for g in range(4 * r, 4 * r + 4, 2):
                    act.wait_ge(g_summed, GROUPS * t + g + 1)
                    if g == 0:
                        wait(act, r1_copied, t)
                    act.copy(gt[:, :, g * GB:(g + 1) * GB],
                             gps[g % 2][:, 0:GB * MX].rearrange("n (b m) -> n m b", b=GB)).then_inc(g_even, 1)

            def step(j, u):
                t = 2 * j + u
                for q in range(QUARTERS):
                    i = QUARTERS * t + q
                    if q == 1 and live(j, u, 2):
                        act.wait_ge(g_odd, 8 * (t - 1))
                        wait(act, g_even, 8 * (t - 1))
                        wait(act, h1_summed, t - 2)
                        act.copy(r1[:], gt[:, FIELDS, :]).then_inc(r1_copied, 1)
                    if live(j, u, 0):
                        for c in range(FILLS):
                            act.wait_ge(z_turned, FILLS * i + c + 1)
                            if c == 0:
                                wait(act, x1_summed, i - 1)
                            src = zps[(FILLS * q + c) % ZBANKS]
                            if c < CHUNKS:
                                act.copy(zt[q % 2][:, c, :], src[:]).then_inc(zt_copied, 1)
                            else:
                                act.copy(ztrest[q % 2][:], src[0:3 * RROWS, :]).then_inc(zt_copied, 1)
                    if live(j, u, 0 if q else 1):
                        act.wait_ge(x1_summed, i)
                        if q == 1:
                            wait(act, x1_turned, 4 * t)
                        k = (q - 1) % QUARTERS
                        act.copy(x1t[:, :, k * DQ:(k + 1) * DQ].rearrange("n b d -> n d b"),
                                 x1ps[:].rearrange("n (d b) -> n d b", d=DQ)
                                 ).then_inc(x1t_copied, 1)
                    if q == 2 and live(j, u, 2):
                        act.wait_ge(h1_summed, t - 1)
                        for k in range(H1 // P):
                            act.activation(h1[:, k, :], mps[:, k * P:(k + 1) * P], ACT.Relu,
                                           bias=b1_sb[:, k:k + 1]).then_inc(h1_made, 1)
                    if q == 3 and live(j, u, 2):
                        act.wait_ge(h2_summed, t - 1)
                        for k in range(H2 // P):
                            act.activation(h2[:, k, :], mps[:, k * P:(k + 1) * P], ACT.Relu,
                                           bias=b2_sb[:, k:k + 1]).then_inc(h2_made, 1)
                    if q == 0:
                        if live(j, u, 3):
                            act.wait_ge(y_summed, t - 2)
                            act.copy(y_sb[:, bass.ds((t - 3) * P, P)], mps[0:1, 0:P]).then_inc(y_copied, 1)
                        if live(j, u, 2):
                            copy_g(t - 2, 3)
                    elif live(j, u, 1):
                        copy_g(t - 1, q - 1)
                    if q == 2 and live(j, u, -1):
                        lay_out(j + u, 1 - u)

            act.wait_ge(top_in, 16 * 6)
            lay_out(0, 0)
            for j in range(FIRST_PAIR):
                step(j, 0)
                step(j, 1)
            with act.Fori(FIRST_PAIR, LAST_PAIR - 1) as j:
                step(j, 0)
                step(j, 1)
            for j in range(LAST_PAIR - 1, LAST_PAIR + 1):
                step(j, 0)
                step(j, 1)
            step(LAST_PAIR + 1, 0)

        @block.vector
        def _(dve):
            for u in range(2):
                for k in range(3):
                    first = CHUNKS * P + k * RROWS
                    dve.memset(prod[u][:, :, first + REST:first + RROWS], 0.0)
            dve.memset(w0b[0:FIELDS, 0, :], 0.0).then_inc(pads_made, 1)
            dve.memset(w0rest[:], 0.0).then_inc(pads_made, 1)
            dve.memset(w0restb[:], 0.0).then_inc(pads_made, 1)
            dve.wait_ge(w0_in, 16)
            dve.wait_ge(w0b_in, 32)
            dve.wait_ge(pads_made, 3)
            dve.tensor_tensor(w0[:], w0[:], w0b[:], ALU.add).then_inc(w0_made, 1)
            dve.wait_ge(rest_in, 16 * 6)
            dve.tensor_tensor(w0rest[:], w0rest[:], w0restb[:], ALU.add).then_inc(w0_made, 1)
            dve.wait_ge(w0_made, 2)
            dve.tensor_copy(w0restr[:], w0rest[:]).then_inc(w0_made, 1)
            dve.wait_ge(w0_made, 3)
            low = slice(2 * RROWS, 3 * RROWS)
            dve.tensor_tensor(w0restr[low, :], w0rest[low, :], w0restr[low, :], ALU.subtract).then_inc(w0_made, 1)
            for k in range(4):
                dve.wait_ge(dense_turned, k + 1)
                dve.tensor_copy(denset[:, k * 512:(k + 1) * 512], gps[k % 2][0:D, :]).then_inc(dense_copied, 1)

            def products(t, i, q, u):
                dve.wait_ge(xext_made, 2 * t + 2)
                wait(dve, z_turned, FILLS * (i - 1))
                x = xext[u][:, q * DQ:(q + 1) * DQ, 0:FIELDS]
                row, dstep = x.ap[0], x.ap[1]
                fixed = bass.AP(x.tensor, x.offset, [row, dstep, [0, SHIFTS], [1, FIELDS]])
                shifted = bass.AP(x.tensor, x.offset, [row, dstep, [1, SHIFTS], [1, FIELDS]])
                out = prod[q % 2][:, :, 0:PAIRS].rearrange("b d (s m) -> b d s m", s=SHIFTS)
                dve.tensor_tensor(out, fixed, shifted, ALU.mult)
                x = xext[u][:, q * DQ:(q + 1) * DQ, FIELDS - REST:FIELDS]
                fixed = bass.AP(x.tensor, x.offset, [row, dstep, [0, 2], [1, REST]])
                shifted = bass.AP(x.tensor, x.offset + SHIFTS - 1, [row, dstep, [0, 2], [1, REST]])
                out = prod[q % 2][:, :, CHUNKS * P + RROWS:ZROW].rearrange("b d (k r) -> b d k r", k=2)[:, :, :, 0:REST]
                dve.tensor_tensor(out, fixed, shifted, ALU.mult).then_inc(prod_made, 1)

            def copy_g(t, r):
                for g in range(4 * r + 1, 4 * r + 4, 2):
                    dve.wait_ge(g_summed, GROUPS * t + g + 1)
                    if g == 1:
                        wait(dve, r1_copied, t)
                    dve.tensor_copy(gt[:, :, g * GB:(g + 1) * GB],
                                    gps[g % 2][:, 0:GB * MX].rearrange("n (b m) -> n m b", b=GB)).then_inc(g_odd, 1)

            def step(j, u):
                t = 2 * j + u
                for q in range(QUARTERS):
                    i = QUARTERS * t + q
                    if q < QUARTERS - 1 and live(j, u, 0):
                        products(t, i + 1, q + 1, u)
                    if q == QUARTERS - 1 and live(j, u, -1):
                        products(t + 1, i + 1, 0, 1 - u)
                    if live(j, u, 0):
                        dve.wait_ge(zt_copied, FILLS * (i + 1))
                        low = slice(RROWS, 2 * RROWS)
                        rest = ztrest[q % 2]
                        dve.tensor_tensor(rest[low, :], zps[(FILLS * q + CHUNKS) % ZBANKS][low, :], rest[low, :],
                                          ALU.subtract).then_inc(rest_split, 1)
                    if q == 1:
                        if live(j, u, 2):
                            dve.wait_ge(r2_summed, t - 1)
                            dve.tensor_copy(r2[:], mps[:, 0:P]).then_inc(r2_copied, 1)
                        if live(j, u, 1):
                            for k in range(4):
                                dve.wait_ge(x1_turned, 4 * (t - 1) + k + 1)
                                dve.tensor_copy(x1[:, 4 * k:4 * k + 4, :].rearrange("p g n -> p (g n)"),
                                                gps[k % 2][:]).then_inc(x1_copied, 1)
                    if q == 0:
                        if live(j, u, 2):
                            copy_g(t - 2, 3)
                    elif live(j, u, 1):
                        copy_g(t - 1, q - 1)

            products(0, 0, 0, 0)
            for j in range(FIRST_PAIR):
                step(j, 0)
                step(j, 1)
            with dve.Fori(FIRST_PAIR, LAST_PAIR - 1) as j:
                step(j, 0)
                step(j, 1)
            for j in range(LAST_PAIR - 1, LAST_PAIR + 1):
                step(j, 0)
                step(j, 1)
            step(LAST_PAIR + 1, 0)


def kernel(**inputs):
    import numpy as np
    import concourse.bacc as bacc
    from concourse.bass_utils import run_bass_kernel_spmd

    nc = bacc.Bacc("TRN2", target_bir_lowering=False, num_devices=1)
    arrays = {}

    def given(name, array):
        array = np.ascontiguousarray(array)
        arrays[name] = array
        return nc.dram_tensor(name, array.shape, mybir.dt.from_np(array.dtype), kind="ExternalInput").ap()

    shift, field = np.divmod(np.arange(PAIRS), FIELDS)
    other = (field + shift) % FIELDS
    w0_rows = np.asarray(inputs["L0_rec_W0"])
    args = [
        given("ids_in_dram", inputs["ids"]),
        given("dense_in_dram", inputs["dense_ctx"]),
        [given(f"tbl_{f}_dram", inputs[f"tbl_{f}"]) for f in range(FIELDS)],
        given("w0_first_dram", w0_rows[field * FIELDS + other]),
        given("w0_second_dram", w0_rows[(other * FIELDS + field)[FIELDS:]]),
        given("w1_dram", inputs["L0_rec_W1"]),
        given("w_top1_dram", inputs["W_top1"]),
        given("b_top1_dram", np.asarray(inputs["b_top1"]).reshape(-1, P).T),
        given("w_top2_dram", inputs["W_top2"]),
        given("b_top2_dram", np.asarray(inputs["b_top2"]).reshape(-1, P).T),
        given("w_top3_dram", np.asarray(inputs["W_top3"]).reshape(-1, P).T),
    ]
    y = nc.dram_tensor("y_dram", (BATCH, 1), F32, kind="ExternalOutput").ap()
    dlrm_tower(nc, *args, y)
    result = run_bass_kernel_spmd(nc, [arrays], core_ids=[0])
    return result.results[0]["y_dram"]
```

```python
from contextlib import ExitStack

import concourse.bass as bass
from concourse import mybir

F32 = mybir.dt.float32
F32R = mybir.dt.float32r
BF16 = mybir.dt.bfloat16
I32 = mybir.dt.int32
ALU = mybir.AluOpType
ACT = mybir.ActivationFunctionType

P = 128
BATCH, FIELDS, D = 2048, 39, 16
CH = 128
TILES = BATCH // P
QUARTERS = 4
DQ = D // QUARTERS
COLS = DQ * P
SHIFTS = (FIELDS + 1) // 2
PAIRS = SHIFTS * FIELDS
CHUNKS = PAIRS // P
REST = PAIRS - CHUNKS * P
RROWS = 32
PARTS = 3
SEL = CHUNKS * P + 3 * RROWS
GB = P // D
GROUPS = P // GB
MX = FIELDS + 1
ZBANKS = 4
FILLS = CHUNKS + 1
ZRING = 4
H1, H2 = 512, 256
SLOTS = 8
ZBANK = [0, 1, 2, 3, 1, 2, 3]
L2_SLOTS = [(2, k) for k in (5, 6, 7)] + [(q, k) for q in (3, 0) for k in range(8)]
FIRST_PAIR, LAST_PAIR = 2, TILES // 2 - 1


def dlrm_tower(nc, ids, dense_t, tables, select, select_t, w0_first, w0_second, w1, w_top1, b_top1, w_top2, b_top2, w_top3, y):
    with ExitStack() as ctx:
        def sb(name, shape, dt=F32):
            return ctx.enter_context(nc.sbuf_tensor(name, shape, dt))

        def bank(name):
            return ctx.enter_context(nc.psum_tensor(name, [P, 512], F32))

        def sem(name):
            return ctx.enter_context(nc.semaphore(name))

        ids_all = sb("ids_all", [P, TILES, FIELDS], I32)
        ids_tile = [sb(f"ids_tile{u}", [P, FIELDS], I32) for u in range(2)]
        emb = [sb(f"emb{u}", [P, FIELDS, D]) for u in range(2)]
        xr = [sb(f"xr{u}", [P, D, FIELDS]) for u in range(2)]
        xparts = [sb(f"xparts{u}", [P, D, PARTS, FIELDS], BF16) for u in range(2)]
        xrem = sb("xrem", [P, D, FIELDS])
        x3t = [sb(f"x3t{k}", [PARTS * FIELDS, COLS], BF16) for k in range(2)]
        zf = [sb(f"zf{k}", [P, COLS]) for k in range(ZRING)]
        zh = [sb(f"zh{k}", [P, CHUNKS, COLS], F32R) for k in range(2)]
        zl = [sb(f"zl{k}", [P, CHUNKS, COLS], F32R) for k in range(2)]
        zrest = [sb(f"zrest{k}", [3 * RROWS, COLS], F32R) for k in range(2)]
        x1t = sb("x1t", [P, P, D])
        x1 = sb("x1", [P, GROUPS, CH])
        xdiag = sb("xdiag", [P, GROUPS, GB, MX])
        gt = sb("gt", [P, MX, P])
        r1 = sb("r1", [P, P])
        r2 = sb("r2", [P, P])
        h1 = sb("h1", [P, H1 // P, P])
        h2 = sb("h2", [P, H2 // P, P])
        y_tile = [sb(f"y_tile{u}", [1, P]) for u in range(2)]
        w0 = sb("w0", [P, CHUNKS, CH])
        w0b, w0restb = gt[:, 0:CHUNKS, :], gt[0:3 * RROWS, CHUNKS, :]
        w0rest = sb("w0rest", [3 * RROWS, CH])
        w0h = sb("w0h", [P, CHUNKS, CH], F32R)
        w0l = sb("w0l", [P, CHUNKS, CH], F32R)
        w0restr = sb("w0restr", [3 * RROWS, CH], F32R)
        sel = sb("sel", [PARTS * FIELDS, SEL], BF16)
        selt = sb("selt", [P, FILLS, FIELDS])
        w1_sb = sb("w1_sb", [P, FIELDS, CH])
        wt1 = sb("wt1", [P, 2, H1])
        wt1c = sb("wt1c", [D, H1])
        wt2 = sb("wt2", [P, H1 // P, H2])
        wt3 = sb("wt3", [P, H2 // P, 1])
        b1_sb = sb("b1_sb", [P, H1 // P])
        b2_sb = sb("b2_sb", [P, H2 // P])
        denset = sb("denset", [D, P])
        ident = sb("ident", [P, P])
        identb = sb("identb", [P, P], BF16)
        carrier = sb("carrier", [1, 1])
        xrows = nc.dram_tensor("xrows", [TILES, P, D, FIELDS], F32, kind="Internal").ap()

        zps = [bank(f"zps{k}") for k in range(ZBANKS)]
        x1ps = bank("x1ps")
        gps = [bank(f"gps{k}") for k in range(2)]
        mps = bank("mps")

        ids_in = sem("ids_in")
        ids_copied = sem("ids_copied")
        ident_made = sem("ident_made")
        diag_made = sem("diag_made")
        w0_in, w0b_in, rest_in = sem("w0_in"), sem("w0b_in"), sem("rest_in")
        sel_in = sem("sel_in")
        w1_in, top_in = sem("w1_in"), sem("top_in")
        dense_in = sem("dense_in")
        pads_made = sem("pads_made")
        w0_made = sem("w0_made")
        emb_in = [sem(f"emb_in{u}") for u in range(2)]
        w0_halved, diag_summed, identb_made = sem("w0_halved"), sem("diag_summed"), sem("identb_made")
        xr_made = sem("xr_made")
        xhigh_made, xrem_made, xmid_made, xlow_made = sem("xhigh_made"), sem("xrem_made"), sem("xmid_made"), sem("xlow_made")
        rows_out = [sem(f"rows_out{u}") for u in range(2)]
        diag_in = [sem(f"diag_in{h}") for h in range(2)]
        x_turned, x3t_copied = sem("x_turned"), sem("x3t_copied")
        s_summed = sem("s_summed")
        squared = sem("squared")
        high_made, low_made = sem("high_made"), sem("low_made")
        x1_summed = sem("x1_summed")
        x1t_copied = sem("x1t_copied")
        x1_turned = sem("x1_turned")
        x1_copied = sem("x1_copied")
        g_summed = sem("g_summed")
        g_even, g_odd = sem("g_even"), sem("g_odd")
        r1_copied = sem("r1_copied")
        r2_summed, r2_copied = sem("r2_summed"), sem("r2_copied")
        h1_summed, h1_made = sem("h1_summed"), sem("h1_made")
        h2_summed, h2_made = sem("h2_summed"), sem("h2_made")
        y_summed, y_copied = sem("y_summed"), sem("y_copied")
        y_out = [sem(f"y_out{u}") for u in range(2)]

        def live(j, u, back):
            return not isinstance(j, int) or 0 <= 2 * j + u - back < TILES

        def wait(eng, semaphore, value):
            if not isinstance(value, int) or value > 0:
                eng.wait_ge(semaphore, value)

        def run(eng, step):
            for j in range(FIRST_PAIR):
                step(j, 0)
                step(j, 1)
            with eng.Fori(FIRST_PAIR, LAST_PAIR) as j:
                step(j, 0)
                step(j, 1)
            for j in range(LAST_PAIR, LAST_PAIR + 2):
                step(j, 0)
                step(j, 1)

        block = ctx.enter_context(nc.Block())

        @block.sync
        def _(sp):
            sp.dma_start(ids_all[:], ids.rearrange("(t p) f -> p t f", p=P)).then_inc(ids_in, 16)
            sp.dma_start(w0[:], w0_first[0:CHUNKS * P, :].rearrange("(c k) n -> k c n", k=P)).then_inc(w0_in, 16)
            sp.dma_start(w0b[FIELDS:P, 0, :], w0_second[0:P - FIELDS, :]).then_inc(w0b_in, 16)
            sp.dma_start(w0b[:, 1:CHUNKS, :], w0_second[P - FIELDS:CHUNKS * P - FIELDS, :]
                         .rearrange("(c k) n -> k c n", k=P)).then_inc(w0b_in, 16)
            sp.dma_start(sel[:], select).then_inc(sel_in, 16)
            sp.dma_start(selt[:], select_t).then_inc(sel_in, 16)
            sp.wait_ge(pads_made, 3)
            for k in range(3):
                rows = slice(k * RROWS, k * RROWS + REST)
                sp.dma_start(w0rest[rows, :], w0_first[CHUNKS * P:PAIRS, :]).then_inc(rest_in, 16)
                sp.dma_start(w0restb[rows, :], w0_second[CHUNKS * P - FIELDS:PAIRS - FIELDS, :]).then_inc(rest_in, 16)
            sp.dma_start(wt1[:], w_top1[0:2 * CH, :].rearrange("(c k) n -> k c n", k=P)).then_inc(top_in, 16)
            sp.dma_start(wt1c[:], w_top1[2 * CH:2 * CH + D, :]).then_inc(top_in, 16)
            sp.dma_start(wt2[:], w_top2.rearrange("(c k) n -> k c n", k=P)).then_inc(top_in, 16)
            sp.dma_start(wt3[:].rearrange("k c n -> k (c n)"), w_top3).then_inc(top_in, 16)
            sp.dma_start(b1_sb[:], b_top1).then_inc(top_in, 16)
            sp.dma_start(b2_sb[:], b_top2).then_inc(top_in, 16)
            sp.dma_start(w1_sb[:], w1.rearrange("(m n) o -> n m o", m=FIELDS)).then_inc(w1_in, 16)
            sp.wait_ge(diag_made, 4)
            blocks = xrows.rearrange("t (g e) d m -> t e d g m", e=GB)

            def step(j, u):
                t = 2 * j + u
                if live(j, u, 0):
                    sp.wait_ge(xr_made, t + 1)
                    sp.dma_start(xrows[bass.ds(t, 1), :, :, :].rearrange("t p d m -> (t p) d m"),
                                 xr[u][:]).then_inc(rows_out[u], 16)
                    sp.wait_ge(rows_out[u], 16 * j + 16)
                    for h in range(2):
                        if live(j, u, 1):
                            sp.wait_ge(g_summed, GROUPS * (t - 1) + (h + 1) * (GROUPS // 2))
                        half = slice(h * (GROUPS // 2), (h + 1) * (GROUPS // 2))
                        for e in range(GB):
                            sp.dma_start(xdiag[e * D:(e + 1) * D, half, e, 0:FIELDS],
                                         blocks[bass.ds(t, 1), e, :, half, :].rearrange("t d g m -> (t d) g m")
                                         ).then_inc(diag_in[h], 16)
            run(sp, step)
            for u in range(2):
                sp.wait_ge(y_out[u], 16 * TILES // 2)

        @block.gpsimd
        def _(pool):
            pool.memset(ident[:], 0.0).then_inc(ident_made, 1)
            pool.wait_ge(ident_made, 1)
            pool.affine_select(out=ident[:], in_=ident[:], compare_op=ALU.not_equal, fill=1.0, base=0,
                               pattern=[[-1, P]], channel_multiplier=1).then_inc(ident_made, 1)
            pool.wait_ge(ids_in, 16)

            def gather(t, u):
                pool.tensor_copy(ids_tile[u][:], ids_all[:, t, :]).then_inc(ids_copied, 1)
                pool.wait_ge(ids_copied, t + 1)
                for f in range(FIELDS):
                    pool.indirect_dma_start(emb[u][:, f, :], None, tables[f],
                                            bass.IndirectOffsetOnAxis(ap=ids_tile[u][:, f:f + 1], axis=0)
                                            ).then_inc(emb_in[u], 16)

            gather(0, 0)
            pool.memset(xdiag[:], 0.0).then_inc(diag_made, 1)
            pool.wait_ge(diag_made, 1)
            ones = xdiag[:, :, :, FIELDS]
            pool.memset(ones, 1.0).then_inc(diag_made, 1)
            pool.wait_ge(diag_made, 2)
            pool.affine_select(out=ones, in_=ones, compare_op=ALU.is_ge, fill=0.0, base=0,
                               pattern=[[0, GROUPS], [-D, GB]], channel_multiplier=1).then_inc(diag_made, 1)
            pool.wait_ge(diag_made, 3)
            pool.affine_select(out=ones, in_=ones, compare_op=ALU.is_ge, fill=0.0, base=D - 1,
                               pattern=[[0, GROUPS], [D, GB]], channel_multiplier=-1).then_inc(diag_made, 1)
            gather(1, 1)
            with pool.Fori(1, TILES // 2) as j:
                for u in range(2):
                    t = 2 * j + u
                    pool.wait_ge(xr_made, t - 1)
                    pool.tensor_copy(ids_tile[u][:], ids_all[:, bass.ds(t, 1), :]
                                     .rearrange("p t f -> p (t f)")).then_inc(ids_copied, 1)
                    pool.wait_ge(ids_copied, t + 1)
                    pool.tensor_tensor(carrier[:], ident[0:1, 0:1], ident[0:1, 0:1], ALU.mult)
                    for f in range(FIELDS):
                        pool.indirect_dma_start(emb[u][:, f, :], None, tables[f],
                                                bass.IndirectOffsetOnAxis(ap=ids_tile[u][:, f:f + 1], axis=0)
                                                ).then_inc(emb_in[u], 16)

        @block.tensor
        def _(pe):
            pe.wait_ge(w0_halved, 2)
            pe.wait_ge(sel_in, 32)
            for c in range(CHUNKS):
                pe.matmul(mps[0:FIELDS, 0:CH], selt[:, c, :], w0[:, c, :], start=(c == 0), stop=False)
            pe.matmul(mps[0:FIELDS, 0:CH], selt[0:3 * RROWS, CHUNKS, :], w0rest[:], start=False, stop=True
                      ).then_inc(diag_summed, 1)
            pe.wait_ge(identb_made, 1)
            pe.wait_ge(w0_made, 5)
            pe.wait_ge(w1_in, 16)
            pe.wait_ge(top_in, 16 * 6)

            def turn_x(t, q, u):
                pe.wait_ge(xlow_made, t + 1)
                for d in range(DQ):
                    src = xparts[u][:, q * DQ + d, :, :].rearrange("b k m -> b (k m)")
                    last = pe.transpose(zps[0][0:PARTS * FIELDS, d * (P // 2):(d + 1) * (P // 2)].bitcast(BF16),
                                        src, identb[:])
                last.then_inc(x_turned, 1)

            def sum_pairs(i, q, c):
                if c == 0:
                    pe.wait_ge(x3t_copied, i + 1)
                elif c < ZBANKS:
                    wait(pe, squared, FILLS * (i - 1) + c + 4)
                else:
                    pe.wait_ge(squared, FILLS * i + c - 2)
                rows = P if c < CHUNKS else 3 * RROWS
                pe.matmul(zps[ZBANK[c]][0:rows, :], sel[:, c * P:c * P + rows], x3t[q % 2][:],
                          start=True, stop=True).then_inc(s_summed, 1)

            def layer1(i, q, c):
                if c == 0:
                    pe.wait_ge(low_made, FILLS * (i + 1))
                    wait(pe, x1t_copied, i)
                if c < CHUNKS:
                    pe.matmul(x1ps[:], w0h[:, c, :], zh[q % 2][:, c, :], start=(c == 0), stop=False)
                    pe.matmul(x1ps[:], w0h[:, c, :], zl[q % 2][:, c, :], start=False, stop=False)
                    pe.matmul(x1ps[:], w0l[:, c, :], zh[q % 2][:, c, :], start=False, stop=False)
                else:
                    pe.matmul(x1ps[:], w0restr[:], zrest[q % 2][:], start=False, stop=True).then_inc(x1_summed, 1)

            def turn_x1(t, k):
                if k == 0:
                    pe.wait_ge(x1t_copied, QUARTERS * (t + 1))
                if k < 2:
                    wait(pe, g_even if k == 0 else g_odd, 8 * t)
                else:
                    pe.wait_ge(x1_copied, 4 * t + k - 1)
                for a in range(4):
                    g = 4 * k + a
                    last = pe.transpose(gps[k % 2][:, a * CH:(a + 1) * CH],
                                        x1t[:, g * GB:(g + 1) * GB, :].rearrange("n b d -> n (b d)"), ident[:])
                last.then_inc(x1_turned, 1)

            def sum_g(t, pair):
                for g in (2 * pair, 2 * pair + 1):
                    if g % 4 == 0:
                        pe.wait_ge(x1_copied, 4 * t + g // 4 + 1)
                    if g % 8 == 0:
                        pe.wait_ge(diag_in[g // 8], 16 * GB * (t + 1))
                    if g < 2:
                        pe.wait_ge(x1_copied, 4 * t + 3 + g)
                    elif g % 2 == 0:
                        pe.wait_ge(g_even, 8 * t + g // 2)
                    else:
                        pe.wait_ge(g_odd, 8 * t + g // 2)
                    pe.matmul(gps[g % 2][:, 0:GB * MX], x1[:, g, :], xdiag[:, g, :, :].rearrange("p b m -> p (b m)"),
                              start=True, stop=True).then_inc(g_summed, 1)

            def layer2(t, n):
                if n == 0:
                    pe.wait_ge(g_even, 8 * (t + 1))
                    pe.wait_ge(g_odd, 8 * (t + 1))
                    wait(pe, y_copied, t)
                for m in range(n * FIELDS // len(L2_SLOTS), (n + 1) * FIELDS // len(L2_SLOTS)):
                    last = pe.matmul(mps[:, 0:P], w1_sb[:, m, :], gt[:, m, :], start=(m == 0), stop=(m == FIELDS - 1))
                if n == len(L2_SLOTS) - 1:
                    last.then_inc(r2_summed, 1)

            def top1(t, k):
                if k == 0:
                    pe.wait_ge(r1_copied, t + 1)
                    pe.wait_ge(r2_copied, t + 1)
                    pe.wait_ge(dense_in, 16 * (t + 1))
                cols = slice(k * P, (k + 1) * P)
                pe.matmul(mps[:, cols], wt1[:, 0, cols], r1[:], start=True, stop=False)
                pe.matmul(mps[:, cols], wt1[:, 1, cols], r2[:], start=False, stop=False)
                last = pe.matmul(mps[:, cols], wt1c[:, cols], denset[:], start=False, stop=True)
                if k == H1 // P - 1:
                    last.then_inc(h1_summed, 1)

            def top2(t, k):
                if k == 0:
                    pe.wait_ge(h1_made, (H1 // P) * (t + 1))
                cols = slice(k * P, (k + 1) * P)
                for c in range(H1 // P):
                    last = pe.matmul(mps[:, cols], wt2[:, c, cols], h1[:, c, :], start=(c == 0),
                                     stop=(c == H1 // P - 1))
                if k == H2 // P - 1:
                    last.then_inc(h2_summed, 1)

            def top3(t):
                pe.wait_ge(h2_made, (H2 // P) * (t + 1))
                for c in range(H2 // P):
                    last = pe.matmul(mps[0:1, 0:P], wt3[:, c, :], h2[:, c, :], start=(c == 0), stop=(c == H2 // P - 1))
                last.then_inc(y_summed, 1)

            def step(j, u):
                t = 2 * j + u
                for q in range(QUARTERS):
                    i = QUARTERS * t + q
                    for k in range(SLOTS):
                        if k < FILLS and live(j, u, 0):
                            sum_pairs(i, q, k)
                        if k == 3 and live(j, u, 0 if q < QUARTERS - 1 else -1):
                            wait(pe, squared, FILLS * i + 1)
                            if q < QUARTERS - 1:
                                turn_x(t, q + 1, u)
                            else:
                                turn_x(t + 1, 0, 1 - u)
                        if k > 0 and live(j, u, 0 if q else 1):
                            layer1(i - 1, (q - 1) % QUARTERS, k - 1)
                        if (q, k) in L2_SLOTS and live(j, u, 1 if q else 2):
                            layer2(t - 1 if q else t - 2, L2_SLOTS.index((q, k)))
                        if q == 1 and 1 <= k <= 4:
                            if live(j, u, 1):
                                turn_x1(t - 1, k - 1)
                            if live(j, u, 2):
                                top1(t - 2, k - 1)
                        if q == 1 and k >= 5 and live(j, u, 1):
                            sum_g(t - 1, k - 5)
                        if q == 1 and k >= 6 and live(j, u, 2):
                            top2(t - 2, k - 6)
                        if q == 2 and k <= 4 and live(j, u, 1):
                            sum_g(t - 1, k + 3)
                        if q == 2 and k == 2 and live(j, u, 2):
                            top3(t - 2)

            turn_x(0, 0, 0)
            run(pe, step)

        @block.scalar
        def _(act):
            def lay_out(j, u):
                t = 2 * j + u
                act.wait_ge(emb_in[u], 16 * FIELDS * (j + 1))
                wait(act, xlow_made, t - 1)
                wait(act, rows_out[u], 16 * j)
                act.copy(xr[u][:], emb[u][:].rearrange("b m d -> b d m")).then_inc(xr_made, 1)
                act.wait_ge(xr_made, t + 1)
                wait(act, x_turned, QUARTERS * (t - 1))
                act.copy(xparts[u][:, :, 0, :], xr[u][:]).then_inc(xhigh_made, 1)

            def copy_g(t, g):
                act.wait_ge(g_summed, GROUPS * t + g + 1)
                if g == 0:
                    wait(act, r1_copied, t)
                act.copy(gt[:, :, g * GB:(g + 1) * GB],
                         gps[g % 2][:, 0:GB * MX].rearrange("n (b m) -> n m b", b=GB)).then_inc(g_even, 1)

            def square(i, q, c):
                act.wait_ge(s_summed, FILLS * i + c + 1)
                wait(act, low_made, FILLS * i + c + 1 - ZRING)
                rows = P if c < CHUNKS else 3 * RROWS
                act.activation(zf[(FILLS * q + c) % ZRING][0:rows, :], zps[ZBANK[c]][0:rows, :],
                               ACT.Square).then_inc(squared, 1)

            def step(j, u):
                t = 2 * j + u
                for q in range(QUARTERS):
                    i = QUARTERS * t + q
                    for k in range(SLOTS):
                        if k == 0 and live(j, u, 0 if q >= 2 else 1):
                            act.wait_ge(x1_summed, i - 1)
                            if q == 2:
                                wait(act, x1_turned, 4 * t)
                            a = (q - 2) % QUARTERS
                            act.copy(x1t[:, :, a * DQ:(a + 1) * DQ].rearrange("n b d -> n d b"),
                                     x1ps[:].rearrange("n (d b) -> n d b", d=DQ)).then_inc(x1t_copied, 1)
                        if k < FILLS and live(j, u, 0):
                            square(i, q, k)
                        if q == 1 and k >= 5 and live(j, u, 1):
                            copy_g(t - 1, 2 * (k - 5))
                        if q == 1 and k == 5 and live(j, u, 2):
                            act.wait_ge(h1_summed, t - 1)
                            for a in range(H1 // P):
                                act.activation(h1[:, a, :], mps[:, a * P:(a + 1) * P], ACT.Relu,
                                               bias=b1_sb[:, a:a + 1]).then_inc(h1_made, 1)
                        if q == 2 and k == 0 and live(j, u, 2):
                            act.wait_ge(h2_summed, t - 1)
                            for a in range(H2 // P):
                                act.activation(h2[:, a, :], mps[:, a * P:(a + 1) * P], ACT.Relu,
                                               bias=b2_sb[:, a:a + 1]).then_inc(h2_made, 1)
                        if q == 2 and k <= 4 and live(j, u, 1):
                            copy_g(t - 1, 2 * (k + 3))
                        if q == 2 and k == 3 and live(j, u, 2):
                            act.wait_ge(y_summed, t - 1)
                            wait(act, y_out[u], 16 * (j - 1))
                            act.copy(y_tile[u][:], mps[0:1, 0:P]).then_inc(y_copied, 1)
                        if q == 2 and k == 5 and live(j, u, 1):
                            act.wait_ge(g_odd, 8 * t)
                            act.wait_ge(g_even, 8 * t)
                            wait(act, h1_summed, t - 1)
                            act.copy(r1[:], gt[:, FIELDS, :]).then_inc(r1_copied, 1)
                            act.dma_start(denset[:], dense_t[:, bass.ds((t - 1) * P, P)]).then_inc(dense_in, 16)
                        if q == 2 and k == 4 and live(j, u, 2):
                            act.wait_ge(y_copied, t - 1)
                            act.dma_start(y[bass.ds((t - 2) * P, P), :].rearrange("b o -> o b"), y_tile[u][:]
                                          ).then_inc(y_out[u], 16)
                        if q == 2 and k == 7 and live(j, u, -1):
                            lay_out(j + u, 1 - u)

            act.wait_ge(top_in, 16 * 6)
            lay_out(0, 0)
            run(act, step)

        @block.vector
        def _(dve):
            dve.memset(w0b[0:FIELDS, 0, :], 0.0).then_inc(pads_made, 1)
            dve.memset(w0rest[:], 0.0).then_inc(pads_made, 1)
            dve.memset(w0restb, 0.0).then_inc(pads_made, 1)
            dve.wait_ge(ident_made, 2)
            dve.tensor_copy(identb[:], ident[:]).then_inc(identb_made, 1)
            dve.wait_ge(w0_in, 16)
            dve.wait_ge(w0b_in, 32)
            dve.wait_ge(pads_made, 3)
            dve.tensor_tensor(w0[:], w0[:], w0b, ALU.add).then_inc(w0_made, 1)
            dve.wait_ge(rest_in, 16 * 6)
            dve.tensor_tensor(w0rest[:], w0rest[:], w0restb, ALU.add).then_inc(w0_made, 1)
            dve.wait_ge(w0_made, 2)
            dve.tensor_scalar(w0[:], w0[:], 0.5, None, ALU.mult).then_inc(w0_halved, 1)
            dve.tensor_scalar(w0rest[:], w0rest[:], 0.5, None, ALU.mult).then_inc(w0_halved, 1)
            dve.wait_ge(diag_summed, 1)
            dve.scalar_tensor_tensor(out=w0[0:FIELDS, 0, :], in0=w0[0:FIELDS, 0, :], scalar=2.0,
                                     in1=mps[0:FIELDS, 0:CH], op0=ALU.mult, op1=ALU.subtract).then_inc(w0_made, 1)
            dve.wait_ge(w0_made, 3)
            dve.tensor_copy(w0h[:], w0[:])
            dve.tensor_copy(w0restr[:], w0rest[:]).then_inc(w0_made, 1)
            dve.wait_ge(w0_made, 4)
            dve.tensor_tensor(w0l[:], w0[:], w0h[:], ALU.subtract)
            low = slice(2 * RROWS, 3 * RROWS)
            dve.tensor_tensor(w0restr[low, :], w0rest[low, :], w0restr[low, :], ALU.subtract).then_inc(w0_made, 1)
            def split_x(t, u):
                dve.wait_ge(xhigh_made, t + 1)
                wait(dve, x_turned, QUARTERS * (t - 1))
                dve.tensor_tensor(xrem[:], xr[u][:], xparts[u][:, :, 0, :], ALU.subtract).then_inc(xrem_made, 1)
                dve.wait_ge(xrem_made, t + 1)
                dve.tensor_copy(xparts[u][:, :, 1, :], xrem[:]).then_inc(xmid_made, 1)
                dve.wait_ge(xmid_made, t + 1)
                dve.tensor_tensor(xparts[u][:, :, 2, :], xrem[:], xparts[u][:, :, 1, :], ALU.subtract
                                  ).then_inc(xlow_made, 1)

            def copy_x3t(i, q):
                dve.wait_ge(x_turned, i + 1)
                wait(dve, s_summed, FILLS * (i - 1))
                dve.tensor_copy(x3t[q % 2][:], zps[0][0:PARTS * FIELDS, 0:COLS // 2].bitcast(BF16)
                                ).then_inc(x3t_copied, 1)

            def high(i, q, c):
                dve.wait_ge(squared, FILLS * i + c + 1)
                src = zf[(FILLS * q + c) % ZRING]
                if c < CHUNKS:
                    dve.tensor_copy(zh[q % 2][:, c, :], src[:]).then_inc(high_made, 1)
                else:
                    dve.tensor_copy(zrest[q % 2][:], src[0:3 * RROWS, :]).then_inc(high_made, 1)

            def low(i, q, c):
                dve.wait_ge(high_made, FILLS * i + c + 1)
                src = zf[(FILLS * q + c) % ZRING]
                if c < CHUNKS:
                    dve.tensor_tensor(zl[q % 2][:, c, :], src[:], zh[q % 2][:, c, :], ALU.subtract
                                      ).then_inc(low_made, 1)
                else:
                    rows = slice(RROWS, 2 * RROWS)
                    dve.tensor_tensor(zrest[q % 2][rows, :], src[rows, :], zrest[q % 2][rows, :], ALU.subtract
                                      ).then_inc(low_made, 1)

            def copy_g(t, g):
                dve.wait_ge(g_summed, GROUPS * t + g + 1)
                if g == 1:
                    wait(dve, r1_copied, t)
                dve.tensor_copy(gt[:, :, g * GB:(g + 1) * GB],
                                gps[g % 2][:, 0:GB * MX].rearrange("n (b m) -> n m b", b=GB)).then_inc(g_odd, 1)

            def step(j, u):
                t = 2 * j + u
                for q in range(QUARTERS):
                    i = QUARTERS * t + q
                    for k in range(SLOTS):
                        if q == 1 and k == 0 and live(j, u, 2):
                            dve.wait_ge(r2_summed, t - 1)
                            dve.tensor_copy(r2[:], mps[:, 0:P]).then_inc(r2_copied, 1)
                        if k < FILLS and live(j, u, 0):
                            if k == 0:
                                wait(dve, x1_summed, i - 1)
                            high(i, q, k)
                        if k > 0 and live(j, u, 0):
                            low(i, q, k - 1)
                        if k == 4 and live(j, u, 0 if q < QUARTERS - 1 else -1):
                            copy_x3t(i + 1, q + 1)
                        if q == 1 and 1 <= k <= 4 and live(j, u, 1):
                            dve.wait_ge(x1_turned, 4 * (t - 1) + k)
                            dve.tensor_copy(x1[:, 4 * k - 4:4 * k, :].rearrange("p g n -> p (g n)"),
                                            gps[(k - 1) % 2][:]).then_inc(x1_copied, 1)
                        if q == 1 and k >= 5 and live(j, u, 1):
                            copy_g(t - 1, 2 * (k - 5) + 1)
                        if q == 2 and k <= 4 and live(j, u, 1):
                            copy_g(t - 1, 2 * (k + 3) + 1)
                        if q == 2 and k == 7 and live(j, u, -1):
                            split_x(t + 1, 1 - u)

            split_x(0, 0)
            copy_x3t(0, 0)
            run(dve, step)


def kernel(**inputs):
    import numpy as np
    import concourse.bacc as bacc
    from concourse.bass_utils import run_bass_kernel_spmd

    nc = bacc.Bacc("TRN2", target_bir_lowering=False, num_devices=1)
    arrays = {}

    def given(name, array):
        array = np.ascontiguousarray(array)
        arrays[name] = array
        return nc.dram_tensor(name, array.shape, mybir.dt.from_np(array.dtype), kind="ExternalInput").ap()

    shift, field = np.divmod(np.arange(PAIRS), FIELDS)
    other = (field + shift) % FIELDS
    member = np.zeros((FIELDS, PAIRS), np.float32)
    member[field, np.arange(PAIRS)] = 1
    member[other, np.arange(PAIRS)] = 1
    one = np.zeros((FIELDS, SEL), np.float32)
    one[:, :CHUNKS * P] = member[:, :CHUNKS * P]
    for k in range(3):
        one[:, CHUNKS * P + k * RROWS:CHUNKS * P + k * RROWS + REST] = member[:, CHUNKS * P:]
    select = np.tile(one, (PARTS, 1)).astype(mybir.dt.np(BF16))
    select_t = np.zeros((FILLS * P, FIELDS), np.float32)
    select_t[FIELDS:PAIRS] = member[:, FIELDS:].T
    select_t = select_t.reshape(FILLS, P, FIELDS).transpose(1, 0, 2)
    w0_rows = np.asarray(inputs["L0_rec_W0"])
    args = [
        given("ids_in_dram", inputs["ids"]),
        given("dense_t_dram", np.asarray(inputs["dense_ctx"]).T),
        [given(f"tbl_{f}_dram", inputs[f"tbl_{f}"]) for f in range(FIELDS)],
        given("select_dram", select), given("select_t_dram", select_t),
        given("w0_first_dram", w0_rows[field * FIELDS + other]),
        given("w0_second_dram", w0_rows[(other * FIELDS + field)[FIELDS:]]),
        given("w1_dram", inputs["L0_rec_W1"]),
        given("w_top1_dram", inputs["W_top1"]),
        given("b_top1_dram", np.asarray(inputs["b_top1"]).reshape(-1, P).T),
        given("w_top2_dram", inputs["W_top2"]),
        given("b_top2_dram", np.asarray(inputs["b_top2"]).reshape(-1, P).T),
        given("w_top3_dram", np.asarray(inputs["W_top3"]).reshape(-1, P).T),
    ]
    y = nc.dram_tensor("y_dram", (BATCH, 1), F32, kind="ExternalOutput").ap()
    dlrm_tower(nc, *args, y)
    result = run_bass_kernel_spmd(nc, [arrays], core_ids=[0])
    return result.results[0]["y_dram"]
```

```python
from contextlib import ExitStack

import concourse.bass as bass
from concourse import mybir

F32 = mybir.dt.float32
F32R = mybir.dt.float32r
BF16 = mybir.dt.bfloat16
I32 = mybir.dt.int32
ALU = mybir.AluOpType
ACT = mybir.ActivationFunctionType

P = 128
BATCH, FIELDS, D = 2048, 39, 16
CH = 128
TILES = BATCH // P
QUARTERS = 4
DQ = D // QUARTERS
COLS = DQ * P
SHIFTS = (FIELDS + 1) // 2
PAIRS = SHIFTS * FIELDS
CHUNKS = PAIRS // P
REST = PAIRS - CHUNKS * P
RROWS = 32
PARTS = 3
SEL = CHUNKS * P + 3 * RROWS
GB = P // D
GROUPS = P // GB
MX = FIELDS + 1
ZBANKS = 4
FILLS = CHUNKS + 1
ACT_LOW = 4
ZRING = 4
SRING = 8
H1, H2 = 512, 256
SLOTS = 8
ZBANK = [0, 1, 2, 3, 1, 2, 3]
L2_SLOTS = [(2, k) for k in (6, 7)] + [(q, k) for q in (3, 0) for k in range(8)]
SPLIT_X = [(2, 5), (2, 6), (2, 7)]
FIRST_PAIR, LAST_PAIR = 2, TILES // 2 - 1


def dlrm_tower(nc, ids, dense_t, tables, select, select_t, w0_first, w0_second, w1, w_top1, b_top1, w_top2, b_top2, w_top3, y):
    with ExitStack() as ctx:
        def sb(name, shape, dt=F32):
            return ctx.enter_context(nc.sbuf_tensor(name, shape, dt))

        def bank(name):
            return ctx.enter_context(nc.psum_tensor(name, [P, 512], F32))

        def sem(name):
            return ctx.enter_context(nc.semaphore(name))

        ids_all = sb("ids_all", [P, TILES, FIELDS], I32)
        ids_tile = [sb(f"ids_tile{u}", [P, FIELDS], I32) for u in range(2)]
        emb = [sb(f"emb{u}", [P, FIELDS, D]) for u in range(2)]
        xr = sb("xr", [P, D, FIELDS])
        xparts = sb("xparts", [P, D, PARTS, FIELDS], BF16)
        xrem = sb("xrem", [P, D, FIELDS])
        x3t = [sb(f"x3t{k}", [PARTS * FIELDS, COLS], BF16) for k in range(2)]
        zf = [sb(f"zf{k}", [P, COLS]) for k in range(ZRING)]
        zh = sb("zh", [P, SRING, COLS], F32R)
        zl = sb("zl", [P, SRING, COLS], F32R)
        zrest = [sb(f"zrest{k}", [3 * RROWS, COLS], F32R) for k in range(2)]
        x1t = sb("x1t", [P, P, D])
        x1 = sb("x1", [P, 2, GROUPS, CH], F32R)
        xd = sb("xd", [P, GROUPS, MX])
        xdh = sb("xdh", [P, GROUPS, MX], F32R)
        xdl = sb("xdl", [P, GROUPS, MX])
        xdiag = [sb(f"xdiag_{part}", [P, GROUPS, GB, MX], F32R) for part in ("high", "low")]
        mask = sb("mask", [P, GB])
        gt = sb("gt", [P, MX, P])
        r1 = sb("r1", [P, P])
        r2 = sb("r2", [P, P])
        h1 = sb("h1", [P, H1 // P, P])
        h2 = sb("h2", [P, H2 // P, P])
        y_tile = [sb(f"y_tile{u}", [1, P]) for u in range(2)]
        w0 = x1t[:, 0:CHUNKS * CH // D, :].rearrange("p b d -> p (b d)").rearrange("p (c n) -> p c n", c=CHUNKS)
        w0b, w0restb = gt[:, 0:CHUNKS, :], gt[0:3 * RROWS, CHUNKS, :]
        w0rest = x1t[0:3 * RROWS, CHUNKS * CH // D:(CHUNKS + 1) * CH // D, :].rearrange("p b d -> p (b d)")
        w0h = sb("w0h", [P, CHUNKS, CH], F32R)
        w0l = sb("w0l", [P, CHUNKS, CH], F32R)
        w0restr = sb("w0restr", [3 * RROWS, CH], F32R)
        sel = sb("sel", [PARTS * FIELDS, SEL], BF16)
        selt = sb("selt", [P, FILLS, FIELDS])
        w1_sb = sb("w1_sb", [P, FIELDS, CH])
        wt1 = sb("wt1", [P, 2, H1])
        wt1c = sb("wt1c", [3 * RROWS, H1], F32R)
        wt1cf = x1t[0:3 * RROWS, P - H1 // D:P, :].rearrange("p b d -> p (b d)")
        wt2 = sb("wt2", [P, H1 // P, H2])
        wt3 = sb("wt3", [P, H2 // P, 1])
        b1_sb = sb("b1_sb", [P, H1 // P])
        b2_sb = sb("b2_sb", [P, H2 // P])
        densef = sb("densef", [3 * RROWS, P])
        dense = sb("dense", [3 * RROWS, P], F32R)
        ident = sb("ident", [P, P])
        identb = sb("identb", [P, P], BF16)
        carrier = sb("carrier", [1, 1])
        xrows = nc.dram_tensor("xrows", [TILES, P, D, FIELDS], F32, kind="Internal").ap()

        zps = [bank(f"zps{k}") for k in range(ZBANKS)]
        x1ps = bank("x1ps")
        gps = [bank(f"gps{k}") for k in range(2)]
        mps = bank("mps")

        ids_in = sem("ids_in")
        ids_copied = sem("ids_copied")
        ident_made = sem("ident_made")
        mask_made = sem("mask_made")
        w0_in, w0b_in, rest_in = sem("w0_in"), sem("w0b_in"), sem("rest_in")
        sel_in = sem("sel_in")
        w1_in, top_in = sem("w1_in"), sem("top_in")
        dense_in = sem("dense_in")
        pads_made = sem("pads_made")
        dense_w_in, dense_w_high, dense_w_split = sem("dense_w_in"), sem("dense_w_high"), sem("dense_w_split")
        dense_high, dense_low = sem("dense_high"), sem("dense_low")
        w0_made = sem("w0_made")
        emb_in = [sem(f"emb_in{u}") for u in range(2)]
        w0_halved, diag_summed, identb_made = sem("w0_halved"), sem("diag_summed"), sem("identb_made")
        xr_made = sem("xr_made")
        xhigh_made, xrem_made, xmid_made, xlow_made = sem("xhigh_made"), sem("xrem_made"), sem("xmid_made"), sem("xlow_made")
        rows_out = [sem(f"rows_out{u}") for u in range(2)]
        xd_in, xdh_made, xdl_made = sem("xd_in"), sem("xdh_made"), sem("xdl_made")
        diag_high = sem("diag_high")
        diag_low_act, diag_low_dve = sem("diag_low_act"), sem("diag_low_dve")
        x_turned, x3t_copied = sem("x_turned"), sem("x3t_copied")
        s_summed = sem("s_summed")
        squared = sem("squared")
        high_made, low_made = sem("high_made"), sem("low_made")
        x1_summed = sem("x1_summed")
        x1t_copied = sem("x1t_copied")
        x1_turned = sem("x1_turned")
        x1_high, x1_low = sem("x1_high"), sem("x1_low")
        g_summed = sem("g_summed")
        g_even, g_odd = sem("g_even"), sem("g_odd")
        r1_copied = sem("r1_copied")
        r2_summed, r2_copied = sem("r2_summed"), sem("r2_copied")
        h1_summed, h1_made = sem("h1_summed"), sem("h1_made")
        h2_summed, h2_made = sem("h2_summed"), sem("h2_made")
        y_summed, y_copied = sem("y_summed"), sem("y_copied")
        y_out = [sem(f"y_out{u}") for u in range(2)]

        def live(j, u, back):
            return not isinstance(j, int) or 0 <= 2 * j + u - back < TILES

        def wait(eng, semaphore, value):
            if not isinstance(value, int) or value > 0:
                eng.wait_ge(semaphore, value)

        def run(eng, step):
            for j in range(FIRST_PAIR):
                step(j, 0)
                step(j, 1)
            with eng.Fori(FIRST_PAIR, LAST_PAIR) as j:
                step(j, 0)
                step(j, 1)
            for j in range(LAST_PAIR, LAST_PAIR + 2):
                step(j, 0)
                step(j, 1)

        block = ctx.enter_context(nc.Block())

        @block.sync
        def _(sp):
            sp.dma_start(ids_all[:], ids.rearrange("(t p) f -> p t f", p=P)).then_inc(ids_in, 16)
            sp.dma_start(w0, w0_first[0:CHUNKS * P, :].rearrange("(c k) n -> k c n", k=P)).then_inc(w0_in, 16)
            sp.dma_start(w0b[FIELDS:P, 0, :], w0_second[0:P - FIELDS, :]).then_inc(w0b_in, 16)
            sp.dma_start(w0b[:, 1:CHUNKS, :], w0_second[P - FIELDS:CHUNKS * P - FIELDS, :]
                         .rearrange("(c k) n -> k c n", k=P)).then_inc(w0b_in, 16)
            sp.dma_start(sel[:], select).then_inc(sel_in, 16)
            sp.dma_start(selt[:], select_t).then_inc(sel_in, 16)
            sp.wait_ge(pads_made, 5)
            for k in range(3):
                rows = slice(k * RROWS, k * RROWS + REST)
                sp.dma_start(w0rest[rows, :], w0_first[CHUNKS * P:PAIRS, :]).then_inc(rest_in, 16)
                sp.dma_start(w0restb[rows, :], w0_second[CHUNKS * P - FIELDS:PAIRS - FIELDS, :]).then_inc(rest_in, 16)
            sp.dma_start(wt1[:], w_top1[0:2 * CH, :].rearrange("(c k) n -> k c n", k=P)).then_inc(top_in, 16)
            for k in range(3):
                sp.dma_start(wt1cf[k * RROWS:k * RROWS + D, :], w_top1[2 * CH:2 * CH + D, :]).then_inc(dense_w_in, 16)
            sp.dma_start(wt2[:], w_top2.rearrange("(c k) n -> k c n", k=P)).then_inc(top_in, 16)
            sp.dma_start(wt3[:].rearrange("k c n -> k (c n)"), w_top3).then_inc(top_in, 16)
            sp.dma_start(b1_sb[:], b_top1).then_inc(top_in, 16)
            sp.dma_start(b2_sb[:], b_top2).then_inc(top_in, 16)
            sp.dma_start(w1_sb[:], w1.rearrange("(m n) o -> n m o", m=FIELDS)).then_inc(w1_in, 16)

            groups = xrows.rearrange("t (g e) d m -> t (e d) g m", e=GB)

            def step(j, u):
                t = 2 * j + u
                if live(j, u, 0):
                    sp.wait_ge(xr_made, t + 1)
                    sp.dma_start(xrows[bass.ds(t, 1), :, :, :].rearrange("t p d m -> (t p) d m"),
                                 xr[:]).then_inc(rows_out[u], 16)
                    if live(j, u, 1):
                        sp.wait_ge(diag_high, GB * t)
                        sp.wait_ge(xdl_made, t)
                    sp.wait_ge(rows_out[u], 16 * j + 16)
                    sp.dma_start(xd[:, :, 0:FIELDS], groups[bass.ds(t, 1), :, :, :]
                                 .rearrange("t p g m -> (t p) g m")).then_inc(xd_in, 16)
                if live(j, u, 1):
                    wait(sp, dense_low, t - 1)
                    for k in range(3):
                        sp.dma_start(densef[k * RROWS:k * RROWS + D, :], dense_t[:, bass.ds((t - 1) * P, P)]
                                     ).then_inc(dense_in, 16)
                if live(j, u, 2):
                    sp.wait_ge(y_copied, t - 1)
                    sp.dma_start(y[bass.ds((t - 2) * P, P), :].rearrange("b o -> o b"), y_tile[u][:]
                                 ).then_inc(y_out[u], 16)
            run(sp, step)
            for u in range(2):
                sp.wait_ge(y_out[u], 16 * TILES // 2)

        @block.gpsimd
        def _(pool):
            pool.memset(ident[:], 0.0).then_inc(ident_made, 1)
            pool.wait_ge(ident_made, 1)
            pool.affine_select(out=ident[:], in_=ident[:], compare_op=ALU.not_equal, fill=1.0, base=0,
                               pattern=[[-1, P]], channel_multiplier=1).then_inc(ident_made, 1)
            pool.wait_ge(ids_in, 16)

            def gather(t, u):
                pool.tensor_copy(ids_tile[u][:], ids_all[:, t, :]).then_inc(ids_copied, 1)
                pool.wait_ge(ids_copied, t + 1)
                for f in range(FIELDS):
                    pool.indirect_dma_start(emb[u][:, f, :], None, tables[f],
                                            bass.IndirectOffsetOnAxis(ap=ids_tile[u][:, f:f + 1], axis=0)
                                            ).then_inc(emb_in[u], 16)

            gather(0, 0)
            pool.memset(xd[:, :, FIELDS], 1.0).then_inc(mask_made, 1)
            pool.memset(mask[:], 1.0).then_inc(mask_made, 1)
            pool.wait_ge(mask_made, 2)
            pool.affine_select(out=mask[:], in_=mask[:], compare_op=ALU.is_ge, fill=0.0, base=0,
                               pattern=[[-D, GB]], channel_multiplier=1).then_inc(mask_made, 1)
            pool.wait_ge(mask_made, 3)
            pool.affine_select(out=mask[:], in_=mask[:], compare_op=ALU.is_ge, fill=0.0, base=D - 1,
                               pattern=[[D, GB]], channel_multiplier=-1).then_inc(mask_made, 1)
            gather(1, 1)
            with pool.Fori(1, TILES // 2) as j:
                for u in range(2):
                    t = 2 * j + u
                    pool.wait_ge(xr_made, t - 1)
                    pool.tensor_copy(ids_tile[u][:], ids_all[:, bass.ds(t, 1), :]
                                     .rearrange("p t f -> p (t f)")).then_inc(ids_copied, 1)
                    pool.wait_ge(ids_copied, t + 1)
                    pool.tensor_tensor(carrier[:], ident[0:1, 0:1], ident[0:1, 0:1], ALU.mult)
                    for f in range(FIELDS):
                        pool.indirect_dma_start(emb[u][:, f, :], None, tables[f],
                                                bass.IndirectOffsetOnAxis(ap=ids_tile[u][:, f:f + 1], axis=0)
                                                ).then_inc(emb_in[u], 16)

        @block.tensor
        def _(pe):
            pe.wait_ge(w0_halved, 2)
            pe.wait_ge(sel_in, 32)
            for c in range(CHUNKS):
                pe.matmul(mps[0:FIELDS, 0:CH], selt[:, c, :], w0[:, c, :], start=(c == 0), stop=False)
            pe.matmul(mps[0:FIELDS, 0:CH], selt[0:3 * RROWS, CHUNKS, :], w0rest, start=False, stop=True
                      ).then_inc(diag_summed, 1)
            pe.wait_ge(identb_made, 1)
            pe.wait_ge(w0_made, 5)
            pe.wait_ge(dense_w_split, 1)
            pe.wait_ge(w1_in, 16)
            pe.wait_ge(top_in, 16 * 5)

            def turn_x(t, q):
                pe.wait_ge(xlow_made, t + 1)
                for d in range(DQ):
                    src = xparts[:, q * DQ + d, :, :].rearrange("b k m -> b (k m)")
                    last = pe.transpose(zps[0][0:PARTS * FIELDS, d * (P // 2):(d + 1) * (P // 2)].bitcast(BF16),
                                        src, identb[:])
                last.then_inc(x_turned, 1)

            def sum_pairs(i, q, c):
                if c == 0:
                    pe.wait_ge(x3t_copied, i + 1)
                elif c < ZBANKS:
                    wait(pe, squared, FILLS * (i - 1) + c + 4)
                else:
                    pe.wait_ge(squared, FILLS * i + c - 2)
                rows = P if c < CHUNKS else 3 * RROWS
                pe.matmul(zps[ZBANK[c]][0:rows, :], sel[:, c * P:c * P + rows], x3t[q % 2][:],
                          start=True, stop=True).then_inc(s_summed, 1)

            def layer1(i, q, c):
                pe.wait_ge(low_made, FILLS * i + c + 1)
                if c == 0:
                    wait(pe, x1t_copied, i)
                if c < CHUNKS:
                    k = (CHUNKS * q + c) % SRING
                    pe.matmul(x1ps[:], w0h[:, c, :], zh[:, k, :], start=(c == 0), stop=False)
                    pe.matmul(x1ps[:], w0h[:, c, :], zl[:, k, :], start=False, stop=False)
                    pe.matmul(x1ps[:], w0l[:, c, :], zh[:, k, :], start=False, stop=False).then_inc(x1_summed, 1)
                else:
                    pe.matmul(x1ps[:], w0restr[:], zrest[q % 2][:], start=False, stop=True).then_inc(x1_summed, 1)

            def turn_x1(t, k):
                if k == 0:
                    pe.wait_ge(x1t_copied, QUARTERS * (t + 1))
                if k < 2:
                    wait(pe, g_even if k == 0 else g_odd, 8 * t)
                else:
                    pe.wait_ge(x1_low, 4 * t + k - 1)
                for a in range(4):
                    g = 4 * k + a
                    last = pe.transpose(gps[k % 2][:, a * CH:(a + 1) * CH],
                                        x1t[:, g * GB:(g + 1) * GB, :].rearrange("n b d -> n (b d)"), ident[:])
                last.then_inc(x1_turned, 1)

            def sum_g(t, pair):
                for g in (2 * pair, 2 * pair + 1):
                    if g == 0:
                        pe.wait_ge(diag_high, GB * (t + 1))
                        pe.wait_ge(diag_low_act, ACT_LOW * (t + 1))
                        pe.wait_ge(diag_low_dve, (GB - ACT_LOW) * (t + 1))
                    if g % 4 == 0:
                        pe.wait_ge(x1_low, 4 * t + g // 4 + 1)
                    if g < 2:
                        pe.wait_ge(x1_low, 4 * t + 3 + g)
                    elif g % 2 == 0:
                        pe.wait_ge(g_even, 8 * t + g // 2)
                    else:
                        pe.wait_ge(g_odd, 8 * t + g // 2)
                    high, low = [x[:, g, :, :].rearrange("p b m -> p (b m)") for x in xdiag]
                    out = gps[g % 2][:, 0:GB * MX]
                    pe.matmul(out, x1[:, 0, g, :], high, start=True, stop=False)
                    pe.matmul(out, x1[:, 0, g, :], low, start=False, stop=False)
                    pe.matmul(out, x1[:, 1, g, :], high, start=False, stop=True).then_inc(g_summed, 1)

            def layer2(t, n):
                if n == 0:
                    pe.wait_ge(g_even, 8 * (t + 1))
                    pe.wait_ge(g_odd, 8 * (t + 1))
                    wait(pe, y_copied, t)
                for m in range(n * FIELDS // len(L2_SLOTS), (n + 1) * FIELDS // len(L2_SLOTS)):
                    last = pe.matmul(mps[:, 0:P], w1_sb[:, m, :], gt[:, m, :], start=(m == 0), stop=(m == FIELDS - 1))
                if n == len(L2_SLOTS) - 1:
                    last.then_inc(r2_summed, 1)

            def top1(t, k):
                if k == 0:
                    pe.wait_ge(r1_copied, t + 1)
                    pe.wait_ge(r2_copied, t + 1)
                    pe.wait_ge(dense_low, t + 1)
                cols = slice(k * P, (k + 1) * P)
                pe.matmul(mps[:, cols], wt1[:, 0, cols], r1[:], start=True, stop=False)
                pe.matmul(mps[:, cols], wt1[:, 1, cols], r2[:], start=False, stop=False)
                last = pe.matmul(mps[:, cols], wt1c[:, cols], dense[:], start=False, stop=True)
                if k == H1 // P - 1:
                    last.then_inc(h1_summed, 1)

            def top2(t, k):
                if k == 0:
                    pe.wait_ge(h1_made, (H1 // P) * (t + 1))
                cols = slice(k * P, (k + 1) * P)
                for c in range(H1 // P):
                    last = pe.matmul(mps[:, cols], wt2[:, c, cols], h1[:, c, :], start=(c == 0),
                                     stop=(c == H1 // P - 1))
                if k == H2 // P - 1:
                    last.then_inc(h2_summed, 1)

            def top3(t):
                pe.wait_ge(h2_made, (H2 // P) * (t + 1))
                for c in range(H2 // P):
                    last = pe.matmul(mps[0:1, 0:P], wt3[:, c, :], h2[:, c, :], start=(c == 0), stop=(c == H2 // P - 1))
                last.then_inc(y_summed, 1)

            def step(j, u):
                t = 2 * j + u
                for q in range(QUARTERS):
                    i = QUARTERS * t + q
                    for k in range(SLOTS):
                        if k < FILLS and live(j, u, 0):
                            sum_pairs(i, q, k)
                        if k == 3 and live(j, u, 0 if q < QUARTERS - 1 else -1):
                            wait(pe, squared, FILLS * i + 1)
                            if q < QUARTERS - 1:
                                turn_x(t, q + 1)
                            else:
                                turn_x(t + 1, 0)
                        if k > 0 and live(j, u, 0 if q else 1):
                            layer1(i - 1, (q - 1) % QUARTERS, k - 1)
                        if (q, k) in L2_SLOTS and live(j, u, 1 if q else 2):
                            layer2(t - 1 if q else t - 2, L2_SLOTS.index((q, k)))
                        if q == 1 and 1 <= k <= 4 and live(j, u, 1):
                            turn_x1(t - 1, k - 1)
                        if q == 1 and 2 <= k <= 5 and live(j, u, 2):
                            top1(t - 2, k - 2)
                        if q == 1 and k >= 5 and live(j, u, 1):
                            sum_g(t - 1, k - 5)
                        if (q, k) in ((1, 7), (2, 0)) and live(j, u, 2):
                            top2(t - 2, q - 1)
                        if q == 2 and k <= 4 and live(j, u, 1):
                            sum_g(t - 1, k + 3)
                        if q == 2 and k == 2 and live(j, u, 2):
                            top3(t - 2)

            turn_x(0, 0)
            run(pe, step)

        @block.scalar
        def _(act):
            def lay_out(j, u):
                t = 2 * j + u
                act.wait_ge(emb_in[u], 16 * FIELDS * (j + 1))
                wait(act, xlow_made, t)
                wait(act, rows_out[1 - u], 16 * (j + u))
                act.copy(xr[:], emb[u][:].rearrange("b m d -> b d m")).then_inc(xr_made, 1)
                act.wait_ge(xr_made, t + 1)
                wait(act, x_turned, QUARTERS * t)
                act.copy(xparts[:, :, 0, :], xr[:]).then_inc(xhigh_made, 1)

            def spread(t, part, e):
                if e == 0:
                    wait(act, g_summed, GROUPS * t)
                    act.wait_ge(mask_made, 4)
                    if part == 0:
                        act.wait_ge(xd_in, 16 * (t + 1))
                    else:
                        act.wait_ge(xdl_made, t + 1)
                act.activation(xdiag[part][:, :, e, :], (xd, xdl)[part][:], ACT.Copy, scale=mask[:, e:e + 1]
                               ).then_inc((diag_high, diag_low_act)[part], 1)

            def copy_g(t, g):
                act.wait_ge(g_summed, GROUPS * t + g + 1)
                if g == 0:
                    wait(act, r1_copied, t)
                act.copy(gt[:, :, g * GB:(g + 1) * GB],
                         gps[g % 2][:, 0:GB * MX].rearrange("n (b m) -> n m b", b=GB)).then_inc(g_even, 1)

            def square(i, q, c):
                act.wait_ge(s_summed, FILLS * i + c + 1)
                wait(act, low_made, FILLS * i + c + 1 - ZRING)
                rows = P if c < CHUNKS else 3 * RROWS
                act.activation(zf[(FILLS * q + c) % ZRING][0:rows, :], zps[ZBANK[c]][0:rows, :],
                               ACT.Square).then_inc(squared, 1)

            def step(j, u):
                t = 2 * j + u
                for q in range(QUARTERS):
                    i = QUARTERS * t + q
                    for k in range(SLOTS):
                        if k == 7 and live(j, u, 0 if q else 1):
                            act.wait_ge(x1_summed, FILLS * i)
                            if q == 1:
                                wait(act, x1_turned, 4 * t)
                            a = (q - 1) % QUARTERS
                            act.copy(x1t[:, :, a * DQ:(a + 1) * DQ].rearrange("n b d -> n d b"),
                                     x1ps[:].rearrange("n (d b) -> n d b", d=DQ)).then_inc(x1t_copied, 1)
                        if q == 1 and k == 0 and live(j, u, 2):
                            act.wait_ge(r2_summed, t - 1)
                            act.copy(r2[:], mps[:, 0:P]).then_inc(r2_copied, 1)
                        if k < FILLS and live(j, u, 0):
                            square(i, q, k)
                        if q == 3 and live(j, u, 0):
                            spread(t, 0, k)
                        if q == 0 and k % 2 == 0 and live(j, u, 1):
                            spread(t - 1, 1, k // 2)
                        if q == 1 and 1 <= k <= 4 and live(j, u, 1):
                            act.wait_ge(x1_turned, 4 * (t - 1) + k)
                            if k == 1:
                                wait(act, g_summed, GROUPS * (t - 1))
                            act.copy(x1[:, 0, 4 * k - 4:4 * k, :].rearrange("p g n -> p (g n)"),
                                     gps[(k - 1) % 2][:]).then_inc(x1_high, 1)
                        if q == 1 and k >= 5 and live(j, u, 1):
                            copy_g(t - 1, 2 * (k - 5))
                        if q == 1 and k == 6 and live(j, u, 2):
                            act.wait_ge(h1_summed, t - 1)
                            for a in range(H1 // P):
                                act.activation(h1[:, a, :], mps[:, a * P:(a + 1) * P], ACT.Relu,
                                               bias=b1_sb[:, a:a + 1]).then_inc(h1_made, 1)
                        if q == 2 and k == 1 and live(j, u, 2):
                            act.wait_ge(h2_summed, t - 1)
                            for a in range(H2 // P):
                                act.activation(h2[:, a, :], mps[:, a * P:(a + 1) * P], ACT.Relu,
                                               bias=b2_sb[:, a:a + 1]).then_inc(h2_made, 1)
                        if q == 2 and k <= 4 and live(j, u, 1):
                            copy_g(t - 1, 2 * (k + 3))
                        if q == 2 and k == 3 and live(j, u, 2):
                            act.wait_ge(y_summed, t - 1)
                            wait(act, y_out[u], 16 * (j - 1))
                            act.copy(y_tile[u][:], mps[0:1, 0:P]).then_inc(y_copied, 1)
                        if q == 2 and k == 6 and live(j, u, 1):
                            act.wait_ge(g_odd, 8 * t)
                            act.wait_ge(g_even, 8 * t)
                            wait(act, h1_summed, t - 1)
                            act.copy(r1[:], gt[:, FIELDS, :]).then_inc(r1_copied, 1)
                        if q == 2 and k == 5 and live(j, u, -1):
                            lay_out(j + u, 1 - u)

            act.wait_ge(top_in, 16 * 5)
            act.wait_ge(w0_made, 5)
            act.wait_ge(dense_w_split, 1)
            lay_out(0, 0)
            run(act, step)

        @block.vector
        def _(dve):
            dve.memset(w0b[0:FIELDS, 0, :], 0.0).then_inc(pads_made, 1)
            dve.memset(w0rest, 0.0).then_inc(pads_made, 1)
            dve.memset(w0restb, 0.0).then_inc(pads_made, 1)
            dve.memset(wt1cf, 0.0).then_inc(pads_made, 1)
            dve.memset(densef[:], 0.0).then_inc(pads_made, 1)
            dve.wait_ge(ident_made, 2)
            dve.tensor_copy(identb[:], ident[:]).then_inc(identb_made, 1)
            dve.wait_ge(w0_in, 16)
            dve.wait_ge(w0b_in, 32)
            dve.wait_ge(pads_made, 5)
            dve.tensor_tensor(w0, w0, w0b, ALU.add).then_inc(w0_made, 1)
            dve.wait_ge(rest_in, 16 * 6)
            dve.tensor_tensor(w0rest, w0rest, w0restb, ALU.add).then_inc(w0_made, 1)
            dve.wait_ge(w0_made, 2)
            dve.tensor_scalar(w0, w0, 0.5, None, ALU.mult).then_inc(w0_halved, 1)
            dve.tensor_scalar(w0rest, w0rest, 0.5, None, ALU.mult).then_inc(w0_halved, 1)
            dve.wait_ge(diag_summed, 1)
            dve.scalar_tensor_tensor(out=w0[0:FIELDS, 0, :], in0=w0[0:FIELDS, 0, :], scalar=2.0,
                                     in1=mps[0:FIELDS, 0:CH], op0=ALU.mult, op1=ALU.subtract).then_inc(w0_made, 1)
            dve.wait_ge(w0_made, 3)
            dve.tensor_copy(w0h[:], w0)
            dve.tensor_copy(w0restr[:], w0rest).then_inc(w0_made, 1)
            dve.wait_ge(w0_made, 4)
            dve.tensor_tensor(w0l[:], w0, w0h[:], ALU.subtract)
            low = slice(2 * RROWS, 3 * RROWS)
            dve.tensor_tensor(w0restr[low, :], w0rest[low, :], w0restr[low, :], ALU.subtract).then_inc(w0_made, 1)
            dve.wait_ge(dense_w_in, 16 * 3)
            dve.tensor_copy(wt1c[:], wt1cf).then_inc(dense_w_high, 1)
            dve.wait_ge(dense_w_high, 1)
            dve.tensor_tensor(wt1c[low, :], wt1cf[low, :], wt1c[low, :], ALU.subtract).then_inc(dense_w_split, 1)

            def split_x(t, part):
                if part == 0:
                    dve.wait_ge(xhigh_made, t + 1)
                    dve.tensor_tensor(xrem[:], xr[:], xparts[:, :, 0, :], ALU.subtract).then_inc(xrem_made, 1)
                elif part == 1:
                    dve.wait_ge(xrem_made, t + 1)
                    dve.tensor_copy(xparts[:, :, 1, :], xrem[:]).then_inc(xmid_made, 1)
                else:
                    dve.wait_ge(xmid_made, t + 1)
                    dve.tensor_tensor(xparts[:, :, 2, :], xrem[:], xparts[:, :, 1, :], ALU.subtract
                                      ).then_inc(xlow_made, 1)

            def copy_x3t(i, q):
                dve.wait_ge(x_turned, i + 1)
                wait(dve, s_summed, FILLS * (i - 1))
                dve.tensor_copy(x3t[q % 2][:], zps[0][0:PARTS * FIELDS, 0:COLS // 2].bitcast(BF16)
                                ).then_inc(x3t_copied, 1)

            def high(i, q, c):
                dve.wait_ge(squared, FILLS * i + c + 1)
                src = zf[(FILLS * q + c) % ZRING]
                if c >= 2 and c < CHUNKS:
                    wait(dve, x1_summed, FILLS * (i - 1) + c - 1)
                elif c < 2:
                    wait(dve, x1_summed, FILLS * (i - 2) + c + 5)
                if c < CHUNKS:
                    dve.tensor_copy(zh[:, (CHUNKS * q + c) % SRING, :], src[:]).then_inc(high_made, 1)
                else:
                    wait(dve, x1_summed, FILLS * (i - 1))
                    dve.tensor_copy(zrest[q % 2][:], src[0:3 * RROWS, :]).then_inc(high_made, 1)

            def low(i, q, c):
                dve.wait_ge(high_made, FILLS * i + c + 1)
                src = zf[(FILLS * q + c) % ZRING]
                if c < CHUNKS:
                    k = (CHUNKS * q + c) % SRING
                    dve.tensor_tensor(zl[:, k, :], src[:], zh[:, k, :], ALU.subtract).then_inc(low_made, 1)
                else:
                    rows = slice(RROWS, 2 * RROWS)
                    dve.tensor_tensor(zrest[q % 2][rows, :], src[rows, :], zrest[q % 2][rows, :], ALU.subtract
                                      ).then_inc(low_made, 1)

            def copy_g(t, g):
                dve.wait_ge(g_summed, GROUPS * t + g + 1)
                if g == 1:
                    wait(dve, r1_copied, t)
                dve.tensor_copy(gt[:, :, g * GB:(g + 1) * GB],
                                gps[g % 2][:, 0:GB * MX].rearrange("n (b m) -> n m b", b=GB)).then_inc(g_odd, 1)

            def step(j, u):
                t = 2 * j + u
                for q in range(QUARTERS):
                    i = QUARTERS * t + q
                    for k in range(SLOTS):
                        if k < FILLS and live(j, u, 0):
                            high(i, q, k)
                        if k > 0 and live(j, u, 0):
                            low(i, q, k - 1)
                        if k == 4 and live(j, u, 0 if q < QUARTERS - 1 else -1):
                            copy_x3t(i + 1, q + 1)
                        if q == 1 and 1 <= k <= 4 and live(j, u, 1):
                            dve.wait_ge(x1_high, 4 * (t - 1) + k)
                            rows = x1[:, :, 4 * k - 4:4 * k, :].rearrange("p k g n -> p k (g n)")
                            dve.tensor_tensor(rows[:, 1, :], gps[(k - 1) % 2][:], rows[:, 0, :], ALU.subtract
                                              ).then_inc(x1_low, 1)
                        if q == 1 and k >= 5 and live(j, u, 1):
                            copy_g(t - 1, 2 * (k - 5) + 1)
                        if q == 2 and k <= 4 and live(j, u, 1):
                            copy_g(t - 1, 2 * (k + 3) + 1)
                        if q == 0 and k % 2 == 1 and live(j, u, 1):
                            e = ACT_LOW + k // 2
                            dve.wait_ge(xdl_made, t)
                            wait(dve, g_summed, GROUPS * (t - 1))
                            dve.wait_ge(mask_made, 4)
                            dve.tensor_scalar(xdiag[1][:, :, e, :], xdl[:], mask[:, e:e + 1], None, ALU.mult
                                              ).then_inc(diag_low_dve, 1)
                        if q == 3 and k == 0 and live(j, u, 1):
                            rows = slice(RROWS, 2 * RROWS)
                            dve.wait_ge(dense_in, 16 * 3 * t)
                            wait(dve, h1_summed, t - 1)
                            dve.tensor_copy(dense[:], densef[:]).then_inc(dense_high, 1)
                            dve.wait_ge(dense_high, t)
                            dve.tensor_tensor(dense[rows, :], densef[rows, :], dense[rows, :], ALU.subtract
                                              ).then_inc(dense_low, 1)
                        if q == 3 and k == 7 and live(j, u, 0):
                            dve.wait_ge(xd_in, 16 * (t + 1))
                            wait(dve, diag_low_act, ACT_LOW * t)
                            wait(dve, diag_low_dve, (GB - ACT_LOW) * t)
                            dve.tensor_copy(xdh[:], xd[:]).then_inc(xdh_made, 1)
                            dve.wait_ge(xdh_made, t + 1)
                            dve.tensor_tensor(xdl[:], xd[:], xdh[:], ALU.subtract).then_inc(xdl_made, 1)
                        if (q, k) in SPLIT_X and live(j, u, -1):
                            split_x(t + 1, SPLIT_X.index((q, k)))

            for part in range(PARTS):
                split_x(0, part)
            copy_x3t(0, 0)
            run(dve, step)


def kernel(**inputs):
    import numpy as np
    import concourse.bacc as bacc
    from concourse.bass_utils import run_bass_kernel_spmd

    nc = bacc.Bacc("TRN2", target_bir_lowering=False, num_devices=1)
    arrays = {}

    def given(name, array):
        array = np.ascontiguousarray(array)
        arrays[name] = array
        return nc.dram_tensor(name, array.shape, mybir.dt.from_np(array.dtype), kind="ExternalInput").ap()

    shift, field = np.divmod(np.arange(PAIRS), FIELDS)
    other = (field + shift) % FIELDS
    member = np.zeros((FIELDS, PAIRS), np.float32)
    member[field, np.arange(PAIRS)] = 1
    member[other, np.arange(PAIRS)] = 1
    one = np.zeros((FIELDS, SEL), np.float32)
    one[:, :CHUNKS * P] = member[:, :CHUNKS * P]
    for k in range(3):
        one[:, CHUNKS * P + k * RROWS:CHUNKS * P + k * RROWS + REST] = member[:, CHUNKS * P:]
    select = np.tile(one, (PARTS, 1)).astype(mybir.dt.np(BF16))
    select_t = np.zeros((FILLS * P, FIELDS), np.float32)
    select_t[FIELDS:PAIRS] = member[:, FIELDS:].T
    select_t = select_t.reshape(FILLS, P, FIELDS).transpose(1, 0, 2)
    w0_rows = np.asarray(inputs["L0_rec_W0"])
    args = [
        given("ids_in_dram", inputs["ids"]),
        given("dense_t_dram", np.asarray(inputs["dense_ctx"]).T),
        [given(f"tbl_{f}_dram", inputs[f"tbl_{f}"]) for f in range(FIELDS)],
        given("select_dram", select), given("select_t_dram", select_t),
        given("w0_first_dram", w0_rows[field * FIELDS + other]),
        given("w0_second_dram", w0_rows[(other * FIELDS + field)[FIELDS:]]),
        given("w1_dram", inputs["L0_rec_W1"]),
        given("w_top1_dram", inputs["W_top1"]),
        given("b_top1_dram", np.asarray(inputs["b_top1"]).reshape(-1, P).T),
        given("w_top2_dram", inputs["W_top2"]),
        given("b_top2_dram", np.asarray(inputs["b_top2"]).reshape(-1, P).T),
        given("w_top3_dram", np.asarray(inputs["W_top3"]).reshape(-1, P).T),
    ]
    y = nc.dram_tensor("y_dram", (BATCH, 1), F32, kind="ExternalOutput").ap()
    dlrm_tower(nc, *args, y)
    result = run_bass_kernel_spmd(nc, [arrays], core_ids=[0])
    return result.results[0]["y_dram"]
```
